# Optimizing a Trainium2 kernel written in Bass

```python
import numpy as np
import jax
import jax.numpy as jnp

def _softmax(x, axis=-1):
    return jax.nn.softmax(x, axis=axis)

def _gelu(x):
    return jax.nn.gelu(x, approximate=True)

def _silu(x):
    return jax.nn.silu(x)

def _sigmoid(x):
    return jax.nn.sigmoid(x)

def _layernorm(x, axis=-1, eps=1e-05):
    m = jnp.mean(x, axis=axis, keepdims=True)
    v = jnp.var(x, axis=axis, keepdims=True)
    return (x - m) / jnp.sqrt(v + eps)

def _scatter_add(tgt, idx, src, axis=0):
    return tgt.at[idx].add(src)

def _segment_sum(src, seg, n):
    return jax.ops.segment_sum(src, seg, n)
kernel_name = 'mk_hybrid_d1_jaxref_r8_eafee8'

def setup_inputs(seed: int=0):
    np.random.seed(seed)
    _w = jnp.asarray

    def _L0_attn_a_setup():
        import jax, jax.numpy as jnp
        import numpy as np
        K_FACTOR = 0.5
        key = jax.random.key(seed)
        k1, k2, k3, k4 = jax.random.split(key, 4)
        B, S, H, I = (1, 256, 512, 1376)
        x = jax.random.normal(k1, (B, S, H), dtype=jnp.float32)
        w_gate = jax.random.normal(k2, (I, H), dtype=jnp.float32) * 0.02
        w_up = jax.random.normal(k3, (I, H), dtype=jnp.float32) * 0.02
        w_down = jax.random.normal(k4, (H, I), dtype=jnp.float32) * 0.02
        return {'x': x, 'w_gate': w_gate, 'w_up': w_up, 'w_down': w_down}
    _L0_attn_a_in = _L0_attn_a_setup()

    def _L0_attn_b_setup():
        import jax, jax.numpy as jnp
        import numpy as np
        HEADS = 32
        key = jax.random.key(seed)
        ks = jax.random.split(key, 5)
        H = 512
        B, S = (2, 256)
        w_scale = 1.0 / np.sqrt(H)
        return {'x': jax.random.normal(ks[0], (B, S, H), dtype=jnp.float32), 'attn_qkvw': jax.random.normal(ks[1], (H, 3 * H), dtype=jnp.float32) * w_scale, 'attn_qkvb': jax.random.normal(ks[2], (3 * H,), dtype=jnp.float32) * 0.02, 'attn_ow': jax.random.normal(ks[3], (H, H), dtype=jnp.float32) * w_scale, 'attn_ob': jax.random.normal(ks[4], (H,), dtype=jnp.float32) * 0.02}
    _L0_attn_b_in = _L0_attn_b_setup()

    def _L0_ffn_setup():
        import jax, jax.numpy as jnp
        import numpy as np
        GROUP_SIZE = 128

        def dequantize(imatrix, scales, zeros, group_size, out_dtype):
            rs = jnp.repeat(scales, group_size, axis=0)
            rz = jnp.repeat(zeros, group_size, axis=0)
            return ((imatrix.astype(rs.dtype) - rz.astype(rs.dtype)) * rs).astype(out_dtype)
        key = jax.random.key(seed)
        ks = jax.random.split(key, 10)
        H, I, G = (512, 1792, GROUP_SIZE)
        B, S = (4, 256)
        x = jax.random.normal(ks[0], (B, S, H), dtype=jnp.float32)
        gate_w = jax.random.randint(ks[1], (H, I), 0, 16, dtype=jnp.int32)
        gate_z = jax.random.randint(ks[2], (H // G, I), 0, 16, dtype=jnp.int32)
        gate_s = jax.random.uniform(ks[3], (H // G, I), dtype=jnp.float32) * 0.01
        up_w = jax.random.randint(ks[4], (H, I), 0, 16, dtype=jnp.int32)
        up_z = jax.random.randint(ks[5], (H // G, I), 0, 16, dtype=jnp.int32)
        up_s = jax.random.uniform(ks[6], (H // G, I), dtype=jnp.float32) * 0.01
        down_w = jax.random.randint(ks[7], (I, H), 0, 16, dtype=jnp.int32)
        down_z = jax.random.randint(ks[8], (I // G, H), 0, 16, dtype=jnp.int32)
        down_s = jax.random.uniform(ks[9], (I // G, H), dtype=jnp.float32) * 0.01
        return {'x': x, 'gate_w': gate_w, 'gate_z': gate_z, 'gate_s': gate_s, 'up_w': up_w, 'up_z': up_z, 'up_s': up_s, 'down_w': down_w, 'down_z': down_z, 'down_s': down_s}
    _L0_ffn_in = _L0_ffn_setup()
    _d = {'L0_attn_a_x': _L0_attn_a_in['x'], 'L0_attn_a_w_gate': _L0_attn_a_in['w_gate'], 'L0_attn_a_w_up': _L0_attn_a_in['w_up'], 'L0_attn_a_w_down': _L0_attn_a_in['w_down'], 'L0_attn_b_attn_qkvw': _L0_attn_b_in['attn_qkvw'], 'L0_attn_b_attn_qkvb': _L0_attn_b_in['attn_qkvb'], 'L0_attn_b_attn_ow': _L0_attn_b_in['attn_ow'], 'L0_attn_b_attn_ob': _L0_attn_b_in['attn_ob'], 'L0_ffn_gate_w': _L0_ffn_in['gate_w'], 'L0_ffn_gate_z': _L0_ffn_in['gate_z'], 'L0_ffn_gate_s': _L0_ffn_in['gate_s'], 'L0_ffn_up_w': _L0_ffn_in['up_w'], 'L0_ffn_up_z': _L0_ffn_in['up_z'], 'L0_ffn_up_s': _L0_ffn_in['up_s'], 'L0_ffn_down_w': _L0_ffn_in['down_w'], 'L0_ffn_down_z': _L0_ffn_in['down_z'], 'L0_ffn_down_s': _L0_ffn_in['down_s']}
    _x0 = _d['L0_attn_a_x']
    _d['L0_attn_a_x'] = jax.random.normal(jax.random.fold_in(jax.random.key(seed), 1), (2, 512, 512), dtype=_x0.dtype)
    del _x0
    return _d

def reference(L0_attn_a_x, L0_attn_a_w_gate, L0_attn_a_w_up, L0_attn_a_w_down, L0_attn_b_attn_qkvw, L0_attn_b_attn_qkvb, L0_attn_b_attn_ow, L0_attn_b_attn_ob, L0_ffn_gate_w, L0_ffn_gate_z, L0_ffn_gate_s, L0_ffn_up_w, L0_ffn_up_z, L0_ffn_up_s, L0_ffn_down_w, L0_ffn_down_z, L0_ffn_down_s):

    def _L0_attn_a_ref(x, w_gate, w_up, w_down):
        import jax, jax.numpy as jnp
        import numpy as np
        K_FACTOR = 0.5
        s = jax.nn.silu(jnp.einsum('bsh,ih->bsi', x, w_gate))
        B, S, I = s.shape
        k = int(K_FACTOR * I)
        _, idx = jax.lax.top_k(-jnp.abs(s), k)
        flat = s.reshape(B * S, I)
        rows = jnp.arange(B * S)[:, None]
        flat = flat.at[rows, idx.reshape(B * S, k)].set(0.0)
        s = flat.reshape(B, S, I)
        s = s * jnp.einsum('bsh,ih->bsi', x, w_up)
        return jnp.einsum('bsi,hi->bsh', s, w_down)

    def _L0_attn_b_ref(x, attn_qkvw, attn_qkvb, attn_ow, attn_ob):
        import jax, jax.numpy as jnp
        import numpy as np
        HEADS = 32
        B, S, H = x.shape
        hd = H // HEADS
        scale = 1.0 / np.sqrt(hd)
        qkv = x @ attn_qkvw + attn_qkvb
        qkv = qkv.reshape(B, S, 3, HEADS, hd)
        q = jnp.transpose(qkv[:, :, 0], (0, 2, 1, 3))
        k = jnp.transpose(qkv[:, :, 1], (0, 2, 1, 3))
        v = jnp.transpose(qkv[:, :, 2], (0, 2, 1, 3))
        scores = jnp.einsum('bhqd,bhkd->bhqk', q, k) * scale
        probs = jax.nn.softmax(scores, axis=-1)
        ctx = jnp.einsum('bhqk,bhkd->bhqd', probs, v)
        ctx = jnp.transpose(ctx, (0, 2, 1, 3)).reshape(B, S, H)
        return ctx @ attn_ow + attn_ob

    def _L0_ffn_ref(x, gate_w, gate_z, gate_s, up_w, up_z, up_s, down_w, down_z, down_s):
        import jax, jax.numpy as jnp
        import numpy as np
        GROUP_SIZE = 128

        def dequantize(imatrix, scales, zeros, group_size, out_dtype):
            rs = jnp.repeat(scales, group_size, axis=0)
            rz = jnp.repeat(zeros, group_size, axis=0)
            return ((imatrix.astype(rs.dtype) - rz.astype(rs.dtype)) * rs).astype(out_dtype)
        dt = x.dtype
        gate_proj = dequantize(gate_w, gate_s, gate_z, GROUP_SIZE, dt)
        up_proj = dequantize(up_w, up_s, up_z, GROUP_SIZE, dt)
        down_proj = dequantize(down_w, down_s, down_z, GROUP_SIZE, dt)
        gate = jax.nn.silu(jnp.dot(x, gate_proj))
        up = jnp.dot(x, up_proj)
        return jnp.dot(gate * up, down_proj)
    x = L0_attn_a_x
    x = x + _L0_attn_a_ref(_layernorm(x, axis=-1), L0_attn_a_w_gate, L0_attn_a_w_up, L0_attn_a_w_down)
    x = x + _L0_ffn_ref(_layernorm(x, axis=-1), L0_ffn_gate_w, L0_ffn_gate_z, L0_ffn_gate_s, L0_ffn_up_w, L0_ffn_up_z, L0_ffn_up_s, L0_ffn_down_w, L0_ffn_down_z, L0_ffn_down_s)
    x = x + _L0_attn_b_ref(_layernorm(x, axis=-1), L0_attn_b_attn_qkvw, L0_attn_b_attn_qkvb, L0_attn_b_attn_ow, L0_attn_b_attn_ob)
    x = x + _L0_ffn_ref(_layernorm(x, axis=-1), L0_ffn_gate_w, L0_ffn_gate_z, L0_ffn_gate_s, L0_ffn_up_w, L0_ffn_up_z, L0_ffn_up_s, L0_ffn_down_w, L0_ffn_down_z, L0_ffn_down_s)
    return x

_drawn_inputs = setup_inputs


def setup_inputs(seed=0):
    import zlib

    import numpy as np

    out = dict(_drawn_inputs(seed))
    spreads = {}
    factors = {'L0_attn_b_attn_qkvb': 3.636, 'L0_attn_b_attn_ob': 3.834}
    for name, (base, spread) in spreads.items():
        noise = np.random.default_rng([zlib.crc32(name.encode()), seed]).standard_normal(out[name].shape)
        drawn = base * np.exp(spread * noise) if base else spread * noise
        out[name] = jnp.asarray(drawn.astype(out[name].dtype))
    for name, factor in factors.items():
        out[name] = (out[name] * factor).astype(out[name].dtype)
    return out
```

```python
from contextlib import ExitStack

import concourse.bass as bass
from concourse import mybir

F32 = mybir.dt.float32
F16 = mybir.dt.float16
I32 = mybir.dt.int32
ALU = mybir.AluOpType
ACT = mybir.ActivationFunctionType
AX = mybir.AxisListType.X

P = 128
EPS = 1e-5
WS = 64.0
HS = 4.0
CS = 8.0
COUNTS = 6
GUESS = 0.785
SLOPE = 0.0016


class Steps:

    def __init__(self, engine, semaphore):
        self.engine, self.semaphore, self.base, self.n = engine, semaphore, 0, 0

    def did(self, instruction):
        instruction.then_inc(self.semaphore, 1)
        self.n += 1

    def settle(self):
        self.engine.wait_ge(self.semaphore, self.base + self.n)


def hybrid_layers(nc, x_in, w_gate_t, w_up_t, w_down_t, qkvw, qkvb, ow, ob,
                  gate_w, gate_z, gate_s, up_w, up_z, up_s, down_w, down_z, down_s, out):
    TOK, H = x_in.shape
    HB = H // P
    TILES = TOK // P
    IA = w_gate_t.shape[1]
    AB = -(-IA // P)
    AR = IA - (AB - 1) * P
    IAP = AB * P
    K_ZERO = IA // 2
    IF = gate_w.shape[1]
    FB = IF // P
    HEADS, HD = 32, 16
    CH = 4
    CT = CH * P
    CHUNKS = TILES // CH
    PAIRS = TILES // 2
    SLOTS = HEADS // 2
    GROUPS = 4
    GS = SLOTS // GROUPS
    LAG = 6
    CW = 256
    QC = IF // CW
    N_GU = 2 * HB * QC
    N_D = FB * (H // CW)
    HD1 = HD + 1
    assert H == 512 and IF % CW == 0 and TILES % CH == 0 and FB % 2 == 0

    ctx = ExitStack()
    with ctx:
        def sb(name, shape, dt):
            return ctx.enter_context(nc.sbuf_tensor(name, shape, dt))

        def sem(name):
            return ctx.enter_context(nc.semaphore(name))

        x = sb("x", [P, TILES, H], F32)
        wa = sb("wa", [P, 4 * HB * IA + 2 * AB * H], F16)
        wf = sb("wf", [P, 4 * HB * IF], F16)
        work = sb("work", [P, 17664], F32)
        ident = sb("ident", [P, P], F32)
        rank8 = sb("rank8", [P, 2, 8], F32)
        bits = sb("bits", [P, 2], I32)
        neg_half = sb("neg_half", [P, TILES], F32)
        bias_qk = sb("bias_qk", [P, 8], F32)
        stats = sb("stats", [P, TILES, 6], F32)
        mean_var = sb("mean_var", [P, TILES, 2], F32)
        var_eps = sb("var_eps", [P, TILES], F32)
        rstd = sb("rstd", [P, TILES], F32)
        recip = sb("recip", [P, 2 * CH], F32)
        sums = sb("sums", [P, PAIRS, 2], F32)
        cur = sb("cur", [P, 4], F32)
        low = sb("low", [P, 4], F32)
        high = sb("high", [P, 4], F32)
        diff = sb("diff", [P, 4], F32)
        take_low = sb("take_low", [P, 4], I32)
        take_high = sb("take_high", [P, 4], I32)
        frac = sb("frac", [P, 2], F32)
        above = sb("above", [P, 2], F32)
        top8 = sb("top8", [P, 2, 8], F32)
        pick8 = sb("pick8", [P, 8], F32)
        thresh = sb("thresh", [P, 2], F32)
        before = sb("before", [P, 2], F32)
        tied = sb("tied", [P, 2], F32)
        bad = sb("bad", [P, 32], F32)
        bad_t = sb("bad_t", [P, 32], F32)
        bad_q = sb("bad_q", [P, 1], F32)
        bad_row = sb("bad_row", [1, 4], F32)
        bad_flag = sb("bad_flag", [1, 1], I32)

        def f16(t, at, *dims):
            n = 1
            for d in dims:
                n *= d
            v = t[:, at:at + n]
            if len(dims) == 2:
                return v.rearrange("p (a b) -> p a b", a=dims[0])
            if len(dims) == 3:
                return v.rearrange("p (a b c) -> p a b c", a=dims[0], b=dims[1])
            return v

        work16 = work[:, :].bitcast(F16)
        work32i = work[:, :].bitcast(I32)
        GA = HB * IA
        ga = [f16(wa, 0, HB, IA), f16(wa, GA, HB, IA)]
        ua = [f16(wa, 2 * GA, HB, IA), f16(wa, 3 * GA, HB, IA)]
        da = [f16(wa, 4 * GA, AB, H), f16(wa, 4 * GA + AB * H, AB, H)]
        at = 2 * FB * H
        fd = [f16(wa, 0, FB, H), f16(wa, FB * H, FB, H)]
        wqkv = [f16(wa, at, HB, 3 * H), f16(wa, at + 3 * HB * H, HB, 3 * H)]
        at += 6 * HB * H
        wo = [f16(wa, at, HB, H), f16(wa, at + HB * H, HB, H)]
        at += 2 * HB * H
        bias_v = f16(wa, at, 2 * H).bitcast(F32)
        bias_o = f16(wa, at + 2 * H, 2 * H).bitcast(F32)
        assert 2 * FB * H <= 4 * GA and at + 4 * H <= 4 * GA + 2 * AB * H
        GF = HB * IF
        fg = [f16(wf, 0, HB, IF), f16(wf, GF, HB, IF)]
        fu = [f16(wf, 2 * GF, HB, IF), f16(wf, 3 * GF, HB, IF)]
        gate_stage = work[:, 0:GA].rearrange("p (a b) -> p a b", a=HB)
        up_stage = work[:, GA:2 * GA].rearrange("p (a b) -> p a b", a=HB)
        DS = 4 * GF - 2 * AB * H
        down_stage = wf[:, DS:4 * GF].bitcast(F32).rearrange("p (a b) -> p a b", a=AB)

        v_abs = work[:, 0:4 * IA].rearrange("p (b j n) -> p b j n", b=2, j=2)
        prod = work[:, 4 * IA:4 * IA + 4 * IAP].rearrange("p (b j n) -> p b j n", b=2, j=2)
        at = 4 * IA + 4 * IAP
        scratch = work[:, at:at + IA]
        scratch16 = f16(work16, 2 * at, 2, IA)
        at += IA
        xa_t = [f16(work16, 2 * at, HB, 2 * P), f16(work16, 2 * at + HB * 2 * P, HB, 2 * P)]
        at += HB * 2 * P
        ha_t = [f16(work16, 2 * at, AB, P), f16(work16, 2 * at + AB * P, AB, P)]
        at += AB * P
        xn_a = work[:, at:at + H]
        at += H
        quant = work[:, at:at + 6 * CW].rearrange("p (b k n) -> p b k n", b=2, k=3)
        quant_i = work32i[:, at:at + 6 * CW].rearrange("p (b k n) -> p b k n", b=2, k=3)
        assert at + 6 * CW <= 17664
        x_t = [f16(work16, 0, HB, CT), f16(work16, HB * CT, HB, CT)]
        at = HB * CT
        h_t = [[f16(work16, 2 * at + (2 * b + s) * CT, CT) for s in range(2)] for b in range(2)]
        at += 2 * CT
        silu_f = [work[:, at + b * CT:at + (b + 1) * CT] for b in range(2)]
        at += 2 * CT
        h_f = [work[:, at + b * CT:at + (b + 1) * CT] for b in range(2)]
        at += 2 * CT
        xn_f = [work[:, at + b * H:at + (b + 1) * H] for b in range(2)]
        at += 2 * H
        attn_stage = work[:, at:at + 4 * HB * H]
        assert at + 4 * HB * H <= 17664
        context = work[:, 0:HB * CT].rearrange("p (i t d) -> p i t d", i=HB, t=CH)
        at = HB * CT
        q_st = f16(work16, 2 * at, SLOTS, CT)
        at += SLOTS * CT // 2
        k_st = f16(work16, 2 * at, SLOTS, CT)
        at += SLOTS * CT // 2
        VW = HEADS * HD1 + 32 - HD1
        v_aug = work[:, at:at + CH * VW].rearrange("p (t n) -> p t n", t=CH)
        v_heads = v_aug[:, :, 0:HEADS * HD1].rearrange("p t (h d) -> p t h d", h=HEADS)
        xn_b = [work[:, at + b * H:at + (b + 1) * H] for b in range(2)]
        qk_full = [work[:, at + (2 + b) * H - 2 * H:at + (3 + b) * H - 2 * H] for b in range(2)]
        at += CH * VW
        probs = work[:, at:at + 2 * CH * CT].rearrange("p (j k n) -> p j k n", j=2, k=CH)
        qk_part = f16(work16, 2 * at, 8, 2, CT)
        at += 2 * CH * CT
        maxima = work[:, at:at + CH * HEADS].rearrange("p (t h) -> p t h", t=CH)
        at += CH * HEADS
        max_rows = f16(work16, 2 * at, CT)
        at += CT // 2
        weighted_t = work[:, at:at + CT]
        at += CT
        weighted = work[:, at:at + 2 * CH * HD1].rearrange("p (t d) -> p t d", d=HD1)
        at += 2 * CH * HD1
        assert at <= 17664

        ps = ctx.enter_context(nc.psum_tensor("ps", [P, 8, 512], F32))
        psf = ps[:, :, :].rearrange("p b n -> p (b n)")
        TR, DO = 6, 7

        x_loaded = [sem(f"x_loaded{i}") for i in range(2)]
        wg_loaded = [sem(f"wg_loaded{i}") for i in range(HB)]
        wu_loaded, wd_loaded, bias_loaded = sem("wu_loaded"), sem("wd_loaded"), sem("bias_loaded")
        attn_w_loaded = sem("attn_w_loaded")
        q_loaded = [sem(f"q_loaded{i}") for i in range(2)]
        const_step, const_ready = sem("const_step"), sem("const_ready")
        wa_hi, wa_lo = sem("wa_hi"), sem("wa_lo")
        q_sub, q_float, q_mul, q_hi, q_lo = (sem(n) for n in ("q_sub", "q_float", "q_mul", "q_hi", "q_lo"))
        aw_scaled, aw_hi, aw_lo = sem("aw_scaled"), sem("aw_hi"), sem("aw_lo")
        pads_zero = sem("pads_zero")
        a_var, a_rstd = sem("a_var"), sem("a_rstd")
        xa_norm, tr_full, tr_hi, tr_lo = sem("xa_norm"), sem("tr_full"), sem("tr_hi"), sem("tr_lo")
        ga_full, ga_silu, ga_abs = sem("ga_full"), sem("ga_silu"), sem("ga_abs")
        ua_full, ua_used = sem("ua_full"), sem("ua_used")
        pruned, da_full, da_added = sem("pruned"), sem("da_full"), sem("da_added")
        sel_step, fallback_step = sem("sel_step"), sem("fallback_step")
        ln_step, ln_var, ln_rstd = sem("ln_step"), sem("ln_var"), sem("ln_rstd")
        ln_norm, ln_full, ln_hi, ln_lo = sem("ln_norm"), sem("ln_full"), sem("ln_hi"), sem("ln_lo")
        gf_full, gf_silu, uf_full, hf_ready = sem("gf_full"), sem("gf_silu"), sem("uf_full"), sem("hf_ready")
        hf_hi, hf_lo, df_done, df_added = sem("hf_hi"), sem("hf_lo"), sem("df_done"), sem("df_added")
        qk_mm, qk_biased, qk_hi, qk_lo = sem("qk_mm"), sem("qk_biased"), sem("qk_hi"), sem("qk_lo")
        stacked, ones_row = sem("stacked"), sem("ones_row")
        v_mm, v_ready, v_ones = sem("v_mm"), sem("v_ready"), sem("v_ones")
        s1_full, max_done, mt_full, mt_ready = sem("s1_full"), sem("max_done"), sem("mt_full"), sem("mt_ready")
        max_moved = [sem(f"max_moved{g}") for g in range(GROUPS)]
        s2_full, exp_done, pv_done = sem("s2_full"), sem("exp_done"), sem("pv_done")
        wt_ready, w_turned, ctx_step, ctx_done = sem("wt_ready"), sem("w_turned"), sem("ctx_step"), sem("ctx_done")
        ct_full, ct_hi, ct_lo, o_full = sem("ct_full"), sem("ct_hi"), sem("ct_lo"), sem("o_full")
        o_step, o_added = sem("o_step"), sem("o_added")
        stored = sem("stored")

        block = ctx.enter_context(nc.Block())

        def quant_chunk(c):
            if c < N_GU:
                m, hb, k = c // (HB * QC), c // QC % HB, c % QC
                w, z, s = ((gate_w, gate_z, gate_s), (up_w, up_z, up_s))[m]
                dst = (fg, fu)[m]
            else:
                hb, k = (c - N_GU) // (H // CW), (c - N_GU) % (H // CW)
                w, z, s, dst = down_w, down_z, down_s, fd
            cols = slice(k * CW, (k + 1) * CW)
            return (w[hb * P:(hb + 1) * P, cols], z[hb:hb + 1, cols].to_broadcast([P, CW]),
                    s[hb:hb + 1, cols].to_broadcast([P, CW]), dst[0][:, hb, cols], dst[1][:, hb, cols])

        @block.sync
        def _(sp):
            xr = x_in.rearrange("(t p) h -> p t h", p=P)
            sp.dma_start(x[:, 0:2, :], xr[:, 0:2, :]).then_inc(x_loaded[0], 16)
            for hb in range(HB):
                sp.dma_start(gate_stage[:, hb, :], w_gate_t[hb * P:(hb + 1) * P, :]).then_inc(wg_loaded[hb], 16)
            sp.dma_start(up_stage, w_up_t.rearrange("(a p) n -> p a n", p=P)).then_inc(wu_loaded, 16)
            sp.dma_start(x[:, 2:TILES, :], xr[:, 2:TILES, :]).then_inc(x_loaded[1], 16)
            full = (AB - 1) * P
            sp.dma_start(down_stage[:, 0:AB - 1, :],
                         w_down_t[0:full, :].rearrange("(a p) n -> p a n", p=P)).then_inc(wd_loaded, 16)
            sp.dma_start(down_stage[0:AR, AB - 1, :], w_down_t[full:IA, :]).then_inc(wd_loaded, 16)
            with nc.allow_non_contiguous_dma(reason="8 bias values of a partition"):
                sp.dma_start(bias_qk[:, :], qkvb[0:2 * H].rearrange("(i p) -> p i", p=P)).then_inc(bias_loaded, 16)
            for c in range(N_GU + N_D):
                w, z, s, _, _ = quant_chunk(c)
                b = c % 2
                if c >= 2:
                    sp.wait_ge(q_sub, c - 1)
                sp.dma_start(quant_i[:, b, 1, :], z).then_inc(q_loaded[b], 16)
                if c >= 2:
                    sp.wait_ge(q_mul, c - 1)
                sp.dma_start(quant_i[:, b, 0, :], w).then_inc(q_loaded[b], 16)
                if c >= 2:
                    sp.wait_ge(q_lo, c - 1)
                sp.dma_start(quant[:, b, 2, :], s).then_inc(q_loaded[b], 16)
            sp.wait_ge(da_added, TILES)
            st = attn_stage.rearrange("p (a n) -> p a n", a=HB)
            sp.dma_start(st[:, :, 0:3 * H], qkvw.rearrange("(a p) n -> p a n", p=P)).then_inc(attn_w_loaded, 16)
            sp.dma_start(st[:, :, 3 * H:4 * H], ow.rearrange("(a p) n -> p a n", p=P)).then_inc(attn_w_loaded, 16)
            sp.dma_start(bias_v, qkvb[2 * H:3 * H].rearrange("(a n) -> a n", a=1).to_broadcast([P, H]))\
              .then_inc(attn_w_loaded, 16)
            sp.dma_start(bias_o, ob.rearrange("(a n) -> a n", a=1).to_broadcast([P, H])).then_inc(attn_w_loaded, 16)

            with sp.Fori(0, CHUNKS) as b:
                for m, (stack, parts) in enumerate(((q_st, (0, 0, 1)), (k_st, (0, 1, 0)))):
                    sp.wait_ge(qk_lo, 8 * b + 4 * m + 4)
                    if m == 1:
                        sp.wait_ge(ones_row, 1)
                    for r, part in enumerate(parts):
                        for j in range(2):
                            for pp in range(4):
                                src = (2 * pp + j) * HD
                                sp.dma_start(stack[64 * j + HD * r:64 * j + HD * (r + 1), pp:SLOTS:4, :],
                                             qk_part[src:src + HD, 4 * m:4 * m + 4, part, :]).then_inc(stacked, 16)
                for g in range(GROUPS):
                    sp.wait_ge(mt_ready, GROUPS * b + g + 1)
                    for j in range(2):
                        sp.dma_start(q_st[64 * j + 48:64 * j + 49, GS * g:GS * (g + 1), :],
                                     max_rows[j:2 * GS:2, :]).then_inc(max_moved[g], 16)

            outr = out.rearrange("(t p) h -> p t h", p=P)
            for t in range(TILES):
                sp.wait_ge(df_added, TILES + t + 1)
                sp.dma_start(outr[:, t, :], x[:, t, :]).then_inc(stored, 16)
            sp.wait_ge(stored, 16 * TILES)

        @block.gpsimd
        def _(pool):
            pool.memset(ident[:, :], 0.0).then_inc(const_step, 1)
            pool.wait_ge(const_step, 1)
            pool.affine_select(out=ident[:, :], in_=ident[:, :], compare_op=ALU.not_equal, fill=1.0, base=0,
                               pattern=[[-1, P]], channel_multiplier=1).then_inc(const_ready, 1)
            pool.memset(neg_half[:, :], -0.5).then_inc(const_step, 1)
            pool.iota(rank8[:, :, :], pattern=[[1, 2], [1, 8]], base=0, channel_multiplier=0,
                      allow_small_or_imprecise_dtypes=True).then_inc(const_ready, 1)
            pool.memset(bad[:, :], 0.0).then_inc(const_ready, 1)

            pool.wait_ge(a_var, 1)
            pool.wait_ge(const_step, 2)
            pool.tensor_tensor(rstd[:, 0:2], var_eps[:, 0:2], neg_half[:, 0:2], ALU.pow).then_inc(a_rstd, 1)
            pool.wait_ge(a_var, 2)
            pool.tensor_tensor(rstd[:, 2:TILES], var_eps[:, 2:TILES], neg_half[:, 2:TILES], ALU.pow)\
                .then_inc(a_rstd, 1)

            for c in range(N_GU + N_D):
                b = c % 2
                _, _, _, hi, lo = quant_chunk(c)
                value_i, value, product = quant_i[:, b, 0, :], quant[:, b, 0, :], quant[:, b, 2, :]
                pool.wait_ge(q_loaded[b], 48 * (c // 2 + 1))
                pool.tensor_tensor(value_i, value_i, quant_i[:, b, 1, :], ALU.subtract).then_inc(q_sub, 1)
                pool.wait_ge(q_sub, c + 1)
                pool.tensor_scalar(value, value_i, WS, 0.0, ALU.mult, ALU.add).then_inc(q_float, 1)
                pool.wait_ge(q_float, c + 1)
                pool.tensor_tensor(product, value, product, ALU.mult).then_inc(q_mul, 1)
                if c == HB * QC:
                    pool.wait_ge(wa_lo, 2 * HB + 2)
                if c == N_GU:
                    pool.wait_ge(ga_full, TILES)
                    pool.wait_ge(ua_full, TILES)
                pool.wait_ge(q_mul, c + 1)
                pool.tensor_scalar(hi, product, 1.0, 0.0, ALU.mult, ALU.add).then_inc(q_hi, 1)
                pool.wait_ge(q_hi, c + 1)
                pool.tensor_tensor(lo, product, hi, ALU.subtract).then_inc(q_lo, 1)

            def ln(i):
                pool.wait_ge(ln_var, i + 1)
                pool.tensor_tensor(rstd[:, 0:CH], var_eps[:, 0:CH], neg_half[:, 0:CH], ALU.pow).then_inc(ln_rstd, 1)

            ln(0)
            pool.wait_ge(attn_w_loaded, 64)
            st = attn_stage.rearrange("p (a n) -> p a n", a=HB)
            for i, (cols, dst) in enumerate(((slice(0, 3 * H), wqkv), (slice(3 * H, 4 * H), wo))):
                pool.tensor_scalar(st[:, :, cols], st[:, :, cols], WS, 0.0, ALU.mult, ALU.add).then_inc(aw_scaled, 1)
                pool.wait_ge(aw_scaled, i + 1)
                pool.tensor_copy(dst[0], st[:, :, cols]).then_inc(aw_hi, 1)
                pool.wait_ge(aw_hi, i + 1)
                pool.tensor_tensor(dst[1], st[:, :, cols], dst[0], ALU.subtract).then_inc(aw_lo, 1)
                if i == 0:
                    ln(1)
            pool.wait_ge(df_added, TILES)
            pool.wait_ge(aw_lo, 2)
            pool.memset(k_st, 1.0).then_inc(ones_row, 1)
            with pool.Fori(0, CHUNKS) as b:
                pool.wait_ge(ln_var, 3 + b)
                pool.tensor_tensor(rstd[:, 0:CH], var_eps[:, 0:CH], neg_half[:, 0:CH], ALU.pow).then_inc(ln_rstd, 1)
                for i in range(8):
                    pool.wait_ge(qk_hi, 8 * b + i + 1)
                    pool.tensor_tensor(qk_part[:, i, 1, :], qk_full[i % 2], qk_part[:, i, 0, :], ALU.subtract)\
                        .then_inc(qk_lo, 1)
            for i in range(4, 6):
                ln(i)

        @block.scalar
        def _(act):
            for hb in range(HB):
                act.wait_ge(wg_loaded[hb], 16)
                act.activation(ga[0][:, hb, :], gate_stage[:, hb, :], ACT.Copy, scale=WS).then_inc(wa_hi, 1)
            act.wait_ge(wu_loaded, 16)
            for hb in range(HB):
                act.activation(ua[0][:, hb, :], up_stage[:, hb, :], ACT.Copy, scale=WS).then_inc(wa_hi, 1)

            def transposed(n, parts, at, width):
                act.wait_ge(tr_full, n + 1)
                act.activation(parts, psf[:, TR * 512 + at:TR * 512 + at + width]
                               .rearrange("p (a q) -> p a q", q=P), ACT.Copy).then_inc(tr_hi, 1)

            fills = [0]

            def fill(parts, width):
                transposed(fills[0], parts, 0, width)
                fills[0] += 1

            for j in range(2):
                fill(xa_t[0][:, :, j * P:(j + 1) * P], H)
            act.wait_ge(wd_loaded, 32)
            act.activation(da[0][:, 0:AB - 1, :], down_stage[:, 0:AB - 1, :], ACT.Copy, scale=WS).then_inc(wa_hi, 1)
            act.activation(da[0][0:AR, AB - 1, :], down_stage[0:AR, AB - 1, :], ACT.Copy, scale=WS).then_inc(wa_hi, 1)
            for n in range(PAIRS + 1):
                if n < PAIRS:
                    for j in range(2):
                        t = 2 * n + j
                        act.wait_ge(ga_full, t + 1)
                        if t >= 4:
                            act.wait_ge(da_full, t - 3)
                        if n == 0:
                            act.wait_ge(wa_lo, 2 * HB)
                        act.activation(prod[:, n % 2, j, 0:IA], psf[:, 0:IA], ACT.Silu, scale=1.0 / WS)\
                            .then_inc(ga_silu, 1)
                        act.wait_ge(ga_silu, t + 1)
                        if n >= 2:
                            act.wait_ge(pruned, t - 3)
                        act.activation(v_abs[:, n % 2, j, :], prod[:, n % 2, j, 0:IA], ACT.Abs,
                                       accum_out=sums[:, n, j:j + 1]).then_inc(ga_abs, 1)
                    if n + 1 < PAIRS:
                        for j in range(2):
                            fill(xa_t[0][:, :, j * P:(j + 1) * P], H)
                if n >= 1:
                    for j in range(2):
                        for k in range(0, AB, 4):
                            w = min(4, AB - k)
                            fill(ha_t[0][:, k:k + w, :], w * P)

            def norm(i):
                for j in range(CH):
                    act.wait_ge(ln_full, CH * i + j + 1)
                    act.activation(x_t[0][:, :, j * P:(j + 1) * P],
                                   ps[:, 4 + j, :].rearrange("p (a q) -> p a q", q=P), ACT.Copy).then_inc(ln_hi, 1)

            def ffn(first):
                with act.Fori(0, CHUNKS) as c:
                    norm(first + c)
                    with act.Fori(0, FB // 2) as k:
                        for b in range(2):
                            m = (first_m(first) + FB * c) + 2 * k + b
                            act.wait_ge(gf_full, m + 1)
                            act.activation(silu_f[b], ps[:, 4 + b, :], ACT.Silu, scale=1.0 / WS).then_inc(gf_silu, 1)
                            act.wait_ge(hf_ready, m + 1)
                            act.activation(h_t[b][0], h_f[b], ACT.Copy).then_inc(hf_hi, 1)

            def first_m(first):
                return 0 if first == 0 else CHUNKS * FB

            ffn(0)
            with act.Fori(0, CHUNKS) as b:
                norm(CHUNKS + b)
                for i in range(8):
                    act.wait_ge(qk_biased, 8 * b + i + 1)
                    act.activation(qk_part[:, i, 0, :], qk_full[i % 2], ACT.Copy).then_inc(qk_hi, 1)

                def exps(s, half):
                    for j in range(2):
                        act.wait_ge(s2_full, 4 * SLOTS * b + 4 * s + 2 * half + j + 1)
                        if s == 0:
                            act.wait_ge(stacked, 768 * b + 768)
                        else:
                            act.wait_ge(pv_done, 2 * SLOTS * b + 2 * (s - 1) + half + 1)
                        act.activation(probs[:, j, 2 * half:2 * half + 2, :],
                                       ps[:, 2 + 2 * j:4 + 2 * j, :], ACT.Exp, scale=HD ** -0.5).then_inc(exp_done, 1)

                def rows(g):
                    act.wait_ge(mt_full, GROUPS * b + g + 1)
                    if g >= 1:
                        act.wait_ge(max_moved[g - 1], 32 * b + 32)
                    act.activation(max_rows[0:2 * GS, :], ps[0:2 * GS, 7, :], ACT.Copy, scale=-1.0)\
                        .then_inc(mt_ready, 1)

                def summed(s):
                    act.wait_ge(pv_done, 2 * SLOTS * b + 2 * s + 2)
                    if s >= 1:
                        act.wait_ge(w_turned, SLOTS * b + s)
                    act.activation(weighted_t, ps[:, 6, :], ACT.Copy).then_inc(wt_ready, 1)

                for u in range(SLOTS + LAG + 1):
                    s = u - LAG
                    if 0 <= s < SLOTS:
                        exps(s, 0)
                    if u >= GS and u % GS == 0 and u // GS <= GROUPS:
                        rows(u // GS - 1)
                    if s >= 1:
                        summed(s - 1)
                    if 0 <= s < SLOTS:
                        exps(s, 1)
                for j in range(CH):
                    act.wait_ge(ct_full, CH * b + CH)
                    act.activation(x_t[0][:, :, j * P:(j + 1) * P],
                                   ps[:, 4 + j, :].rearrange("p (a q) -> p a q", q=P), ACT.Copy).then_inc(ct_hi, 1)
            ffn(2 * CHUNKS)

        @block.vector
        def _(dve):
            sel = Steps(dve, sel_step)

            def statistics(lo, hi):
                for t in range(lo, hi):
                    sel.did(dve.bn_stats(stats[:, t, :], x[:, t, :]))
                sel.settle()
                for t in range(lo, hi):
                    sel.did(dve.bn_aggr(mean_var[:, t, :], stats[:, t, :]))
                sel.settle()
                dve.tensor_scalar(var_eps[:, lo:hi], mean_var[:, lo:hi, 1], EPS, None, ALU.add).then_inc(a_var, 1)

            dve.wait_ge(x_loaded[0], 16)
            statistics(0, 2)
            for hb in range(HB):
                dve.wait_ge(wa_hi, hb + 1)
                dve.scalar_tensor_tensor(ga[1][:, hb, :], gate_stage[:, hb, :], WS, ga[0][:, hb, :],
                                         ALU.mult, ALU.subtract).then_inc(wa_lo, 1)

            def normed(t):
                if t % TILES >= 1:
                    dve.wait_ge(tr_full, x_fill(t - 1) + 1)
                dve.tensor_scalar(xn_a, x[:, t, :], mean_var[:, t, 0:1], rstd[:, t:t + 1],
                                  ALU.subtract, ALU.mult).then_inc(xa_norm, 1)

            def x_fill(t):
                return t if t < 6 else t + 6 * (t // 2 - 2)

            def low_part(n, hi, lo, width):
                dve.wait_ge(tr_hi, n + 1)
                dve.tensor_tensor(lo, psf[:, TR * 512:TR * 512 + width].rearrange("p (a q) -> p a q", q=P), hi,
                                  ALU.subtract).then_inc(tr_lo, 1)

            fills = [0]

            def fill(parts, width):
                low_part(fills[0], parts[0], parts[1], width)
                fills[0] += 1

            dve.wait_ge(a_rstd, 1)
            for j in range(2):
                normed(j)
                fill([q[:, :, j * P:(j + 1) * P] for q in xa_t], H)
            for hb in range(HB):
                dve.wait_ge(wa_hi, HB + hb + 1)
                dve.scalar_tensor_tensor(ua[1][:, hb, :], up_stage[:, hb, :], WS, ua[0][:, hb, :],
                                         ALU.mult, ALU.subtract).then_inc(wa_lo, 1)
            dve.wait_ge(x_loaded[1], 16)
            statistics(2, TILES)
            dve.wait_ge(wa_hi, 2 * HB + 2)
            dve.scalar_tensor_tensor(da[1][:, 0:AB - 1, :], down_stage[:, 0:AB - 1, :], WS, da[0][:, 0:AB - 1, :],
                                     ALU.mult, ALU.subtract).then_inc(wa_lo, 1)
            dve.scalar_tensor_tensor(da[1][0:AR, AB - 1, :], down_stage[0:AR, AB - 1, :], WS, da[0][0:AR, AB - 1, :],
                                     ALU.mult, ALU.subtract).then_inc(wa_lo, 1)
            dve.memset(da[0][AR:P, AB - 1, :], 0.0).then_inc(pads_zero, 1)
            dve.memset(da[1][AR:P, AB - 1, :], 0.0).then_inc(pads_zero, 1)
            dve.wait_ge(wa_lo, 2 * HB)
            dve.memset(prod[:, :, :, IA:IAP], 0.0).then_inc(pads_zero, 1)

            GOAL = K_ZERO + 3.5
            first = [True]

            def twice(v):
                return v.unsqueeze(1).to_broadcast([P, 2, 2])

            def pairs(v):
                return v.rearrange("p (a b) -> p a b", a=2)

            def count(n, it):
                for j in range(2):
                    sel.did(dve.tensor_scalar(scratch16[:, j, :], v_abs[:, n % 2, j, :], cur[:, j:j + 1], None,
                                              ALU.is_le, ALU.add, accum_out=cur[:, 2 + j:3 + j]))
                sel.settle()
                sel.did(dve.tensor_scalar(pairs(take_low[:, :]), twice(cur[:, 2:4]), GOAL, None, ALU.is_lt))
                sel.did(dve.tensor_scalar(pairs(take_high[:, :]), twice(cur[:, 2:4]), GOAL, None, ALU.is_gt))
                sel.settle()
                sel.did(dve.copy_predicated(low[:, :], take_low[:, :], cur[:, :]))
                sel.did(dve.copy_predicated(high[:, :], take_high[:, :], cur[:, :]))
                sel.settle()

            def guess(n, it):
                if it == 0:
                    sel.did(dve.tensor_scalar(frac[:, :], cur[:, 2:4], -SLOPE / IA, SLOPE / IA * GOAL,
                                              ALU.mult, ALU.add))
                    sel.settle()
                    sel.did(dve.tensor_tensor(frac[:, :], frac[:, :], sums[:, n, :], ALU.mult))
                    sel.settle()
                    sel.did(dve.tensor_tensor(cur[:, 0:2], cur[:, 0:2], frac[:, :], ALU.add))
                    sel.settle()
                    return
                sel.did(dve.tensor_tensor(diff[:, :], high[:, :], low[:, :], ALU.subtract))
                sel.did(dve.tensor_scalar(frac[:, :], low[:, 2:4], -1.0, GOAL, ALU.mult, ALU.add))
                sel.settle()
                sel.did(dve.reciprocal(above[:, :], diff[:, 2:4]))
                sel.settle()
                sel.did(dve.tensor_tensor(frac[:, :], frac[:, :], above[:, :], ALU.mult))
                sel.settle()
                sel.did(dve.tensor_tensor(frac[:, :], frac[:, :], diff[:, 0:2], ALU.mult))
                sel.settle()
                sel.did(dve.tensor_tensor(cur[:, 0:2], low[:, 0:2], frac[:, :], ALU.add))
                sel.settle()

            def start(n):
                dve.wait_ge(ga_abs, 2 * n + 2)
                sel.did(dve.memset(low[:, :], 0.0))
                sel.did(dve.tensor_scalar(high[:, 0:2], sums[:, n, :], 8.0 / IA, None, ALU.mult))
                sel.did(dve.memset(high[:, 2:4], float(IA)))
                sel.did(dve.tensor_scalar(cur[:, 0:2], sums[:, n, :], GUESS / IA, None, ALU.mult))
                sel.settle()

            def general(n):
                done = Steps(dve, fallback_step)
                for j in range(2):
                    v = v_abs[:, n % 2, j, :]
                    p = prod[:, n % 2, j, 0:IA]
                    bit, trial = bits[:, 0:1], bits[:, 1:2]
                    found = low[:, j:j + 1]
                    done.did(dve.memset(bit, 1 << 30))
                    done.did(dve.memset(found.bitcast(I32), 0))
                    done.settle()
                    with dve.Fori(0, 31) as i:
                        inner = Steps(dve, fallback_step)
                        inner.base = done.n + 5 * i
                        inner.did(dve.tensor_tensor(trial, found.bitcast(I32), bit, ALU.bitwise_or))
                        inner.settle()
                        inner.did(dve.tensor_scalar(scratch16[:, 0, :], v, trial.bitcast(F32), None, ALU.is_lt, ALU.add,
                                                    accum_out=frac[:, 0:1]))
                        inner.settle()
                        inner.did(dve.tensor_scalar(take_low[:, 0:1], frac[:, 0:1], float(K_ZERO), None, ALU.is_lt))
                        inner.settle()
                        inner.did(dve.tensor_scalar(bit, bit, 1, None, ALU.logical_shift_right))
                        inner.did(dve.copy_predicated(found, take_low[:, 0:1], trial.bitcast(F32)))
                        inner.settle()
                    done.n += 5 * 31
                    done.did(dve.tensor_scalar(scratch16[:, 0, :], v, found, None, ALU.is_lt, ALU.add,
                                               accum_out=frac[:, 0:1]))
                    done.did(dve.tensor_scalar(diff[:, 0:1], found, 1.0, None, ALU.mult))
                    done.settle()
                    done.did(dve.tensor_scalar(frac[:, 0:1], frac[:, 0:1], -1.0, float(K_ZERO), ALU.mult, ALU.add))
                    done.did(dve.tensor_scalar(scratch, v, found, None, ALU.is_equal))
                    done.settle()
                    done.did(dve.tensor_tensor_scan(scratch, scratch, scratch, 0.0, ALU.add, ALU.max))
                    done.settle()
                    done.did(dve.tensor_scalar(scratch, scratch, frac[:, 0:1], None, ALU.is_le))
                    done.settle()
                    done.did(dve.scalar_tensor_tensor(scratch, v, found, scratch, ALU.is_equal, ALU.mult))
                    done.settle()
                    done.did(dve.scalar_tensor_tensor(scratch, v, found, scratch, ALU.is_lt, ALU.add))
                    done.settle()
                    done.did(dve.tensor_scalar(scratch, scratch, -1.0, 1.0, ALU.mult, ALU.add))
                    done.settle()
                    done.did(dve.tensor_tensor(p, p, scratch, ALU.mult))
                    done.did(dve.memset(thresh[:, j:j + 1], -1.0))
                    done.settle()
                dve.sem_clear(fallback_step)

            def finish(n):
                sel.did(dve.tensor_scalar(pairs(take_high[:, :]), twice(high[:, 2:4]), K_ZERO + 7.5, None, ALU.is_lt))
                sel.settle()
                sel.did(dve.copy_predicated(low[:, :], take_high[:, :], high[:, :]))
                sel.settle()
                sel.did(dve.tensor_scalar(above[:, :], low[:, 2:4], -float(K_ZERO), None, ALU.add))
                for j in range(2):
                    v = v_abs[:, n % 2, j, :]
                    sel.did(dve.scalar_tensor_tensor(scratch, v, low[:, j:j + 1], v, ALU.is_le, ALU.mult))
                    sel.settle()
                    sel.did(dve.max(top8[:, j, :], scratch))
                    sel.settle()
                    for k, kept in enumerate((thresh, before)):
                        sel.did(dve.scalar_tensor_tensor(pick8[:, :], rank8[:, k, :], above[:, j:j + 1], top8[:, j, :],
                                                         ALU.is_equal, ALU.mult, accum_out=kept[:, j:j + 1]))
                        sel.settle()
                sel.did(dve.tensor_tensor(tied[:, :], thresh[:, :], before[:, :], ALU.is_equal))
                sel.settle()
                sel.did(dve.tensor_reduce(bad[:, 0:1], tied[:, :], AX, ALU.max))
                sel.settle()
                sel.did(dve.transpose(bad_t[:, :], bad[:, :]))
                sel.settle()
                sel.did(dve.tensor_reduce(bad_q[:, :], bad_t[:, :], AX, ALU.max))
                sel.settle()
                for q in range(4):
                    sel.did(dve.tensor_copy(bad_row[:, q:q + 1], bad_q[32 * q:32 * q + 1, :]))
                sel.settle()
                sel.did(dve.tensor_reduce(bad_flag[:, :], bad_row[:, :], AX, ALU.max))
                sel.settle()
                failed = dve.value_load(bad_flag[0:1, 0:1])
                with dve.If(failed):
                    general(n)

            def select_first(n):
                start(n)
                for it in range(4):
                    count(n, it)
                    guess(n, it)

            def select_last(n):
                for it in range(4, COUNTS):
                    count(n, it)
                    if it + 1 < COUNTS:
                        guess(n, it)
                finish(n)

            def prune(n):
                for j in range(2):
                    p = prod[:, n % 2, j, 0:IA]
                    dve.wait_ge(ua_used, 2 * n + j + 1)
                    dve.scalar_tensor_tensor(p, v_abs[:, n % 2, j, :], thresh[:, j:j + 1], p, ALU.is_gt, ALU.mult)\
                        .then_inc(pruned, 1)

            def product(t):
                n, j = t // 2, t % 2
                p = prod[:, n % 2, j, 0:IA]
                dve.wait_ge(ua_full, t + 1)
                dve.wait_ge(ga_abs, t + 1)
                dve.scalar_tensor_tensor(p, psf[:, 3 * 512:3 * 512 + IA], HS / WS, p, ALU.mult, ALU.mult)\
                    .then_inc(ua_used, 1)

            for n in range(PAIRS + 1):
                if n >= 1:
                    select_first(n - 1)
                if n < PAIRS:
                    product(2 * n)
                if n >= 1:
                    select_last(n - 1)
                    prune(n - 1)
                if n < PAIRS:
                    product(2 * n + 1)
                if n + 1 < PAIRS:
                    dve.wait_ge(a_rstd, 2)
                    for j in range(2):
                        normed(2 * n + 2 + j)
                        fill([q[:, :, j * P:(j + 1) * P] for q in xa_t], H)
                if n >= 1:
                    for j in range(2):
                        for k in range(0, AB, 4):
                            w = min(4, AB - k)
                            fill([q[:, k:k + w, :] for q in ha_t], w * P)
                        t = 2 * n - 2 + j
                        dve.wait_ge(da_full, t + 1)
                        dve.scalar_tensor_tensor(x[:, t, :], ps[:, DO, :], 1.0 / (HS * WS), x[:, t, :],
                                                 ALU.mult, ALU.add).then_inc(da_added, 1)

            def norm(i, c, xn):
                st = Steps(dve, ln_step)
                st.base = (2 * CH + 1) * i
                for j in range(CH):
                    st.did(dve.bn_stats(stats[:, j, :], x[:, bass.ds(CH * c + j, 1), :].rearrange("p a n -> p (a n)")))
                st.settle()
                st.did(dve.memset(var_eps[:, 0:CH], EPS))
                for j in range(CH):
                    st.did(dve.bn_aggr(mean_var[:, j, :], stats[:, j, :]))
                st.settle()
                dve.tensor_tensor(var_eps[:, 0:CH], mean_var[:, 0:CH, 1], var_eps[:, 0:CH], ALU.add).then_inc(ln_var, 1)
                dve.wait_ge(ln_rstd, i + 1)
                for j in range(CH):
                    if j >= 2:
                        dve.wait_ge(ln_full, CH * i + j - 1)
                    dve.tensor_scalar(xn[j % 2], x[:, bass.ds(CH * c + j, 1), :].rearrange("p a n -> p (a n)"),
                                      mean_var[:, j, 0:1], rstd[:, j:j + 1], ALU.subtract, ALU.mult)\
                       .then_inc(ln_norm, 1)
                for j in range(CH):
                    cols = slice(j * P, (j + 1) * P)
                    dve.wait_ge(ln_hi, CH * i + j + 1)
                    dve.tensor_tensor(x_t[1][:, :, cols], ps[:, 4 + j, :].rearrange("p (a q) -> p a q", q=P),
                                      x_t[0][:, :, cols], ALU.subtract).then_inc(ln_lo, 1)

            def ffn(f):
                with dve.Fori(0, CHUNKS) as c:
                    norm(2 * CHUNKS * f + c, c, xn_f)
                    with dve.Fori(0, FB // 2) as k:
                        for b in range(2):
                            m = CHUNKS * FB * f + FB * c + 2 * k + b
                            dve.wait_ge(uf_full, m + 1)
                            dve.wait_ge(gf_silu, m + 1)
                            dve.scalar_tensor_tensor(h_f[b], ps[:, 6 + b, :], HS / WS, silu_f[b], ALU.mult, ALU.mult)\
                               .then_inc(hf_ready, 1)
                            dve.wait_ge(hf_hi, m + 1)
                            dve.tensor_tensor(h_t[b][1], h_f[b], h_t[b][0], ALU.subtract).then_inc(hf_lo, 1)
                    dve.wait_ge(df_done, CHUNKS * FB * f + FB * c + FB)
                    for j in range(CH):
                        xt = x[:, bass.ds(CH * c + j, 1), :].rearrange("p a n -> p (a n)")
                        dve.scalar_tensor_tensor(xt, ps[:, j, :], 1.0 / (HS * WS), xt, ALU.mult, ALU.add)\
                           .then_inc(df_added, 1)

            ffn(0)
            dve.wait_ge(bias_loaded, 16)
            with dve.Fori(0, CHUNKS) as b:
                norm(CHUNKS + b, b, xn_b)
                for i in range(8):
                    dve.wait_ge(qk_mm, 8 * b + i + 1)
                    if i >= 2:
                        dve.wait_ge(qk_lo, 8 * b + i - 1)
                    dve.tensor_scalar(qk_full[i % 2], ps[:, i % 4, :], 1.0 / WS, bias_qk[:, i:i + 1],
                                      ALU.mult, ALU.add).then_inc(qk_biased, 1)
                dve.wait_ge(qk_lo, 8 * b + 8)
                for j in range(CH):
                    dve.wait_ge(v_mm, CH * b + j + 1)
                    dve.scalar_tensor_tensor(v_heads[:, j, :, 0:HD], ps[:, j, :].rearrange("p (h d) -> p h d", h=HEADS),
                                             1.0 / WS, bias_v.rearrange("p (h d) -> p h d", h=HEADS),
                                             ALU.mult, ALU.add).then_inc(v_ready, 1)
                dve.memset(v_heads[:, :, :, HD], 1.0 / CS).then_inc(v_ones, 1)
                dve.memset(v_aug[:, :, HEADS * HD1:VW], 0.0).then_inc(v_ones, 1)

                def maxes(s, qt):
                    if s < SLOTS:
                        for j in range(2):
                            dve.wait_ge(s1_full, 8 * SLOTS * b + 8 * s + 2 * qt + j + 1)
                            dve.tensor_reduce(maxima[:, qt, 2 * s + j:2 * s + j + 1], ps[:, j, :], AX, ALU.max)\
                               .then_inc(max_done, 1)

                def normalise(s):
                    st = Steps(dve, ctx_step)
                    st.base = 3 * SLOTS * b + 3 * s
                    dve.wait_ge(w_turned, SLOTS * b + s + 1)
                    halves = ps[:, 7, :].rearrange("p (t k d) -> p t k d", k=2, d=32)
                    st.did(dve.tensor_copy(weighted, halves[:, :, 1, 0:HD1]))
                    st.settle()
                    st.did(dve.tensor_tensor(weighted, weighted, halves[:, :, 0, 0:HD1], ALU.add))
                    st.settle()
                    st.did(dve.reciprocal(recip[:, :], weighted[:, :, HD]))
                    st.settle()
                    cols = 2 * HD * (s % 4)
                    dst = context[:, s // 4, :, cols:cols + 2 * HD].rearrange("p t (j d) -> p t j d", j=2)
                    dve.tensor_tensor(dst, weighted[:, :, 0:HD].rearrange("p (t j) d -> p t j d", j=2),
                                      recip[:, :].rearrange("p (t j) -> p t j", j=2).unsqueeze(3)
                                      .to_broadcast([P, CH, 2, HD]), ALU.mult).then_inc(ctx_done, 1)

                for u in range(SLOTS + LAG + 1):
                    for qt in range(3):
                        maxes(u, qt)
                    if u > LAG:
                        normalise(u - LAG - 1)
                    maxes(u, 3)
                for j in range(CH):
                    cols = slice(j * P, (j + 1) * P)
                    dve.wait_ge(ct_hi, CH * b + j + 1)
                    dve.tensor_tensor(x_t[1][:, :, cols], ps[:, 4 + j, :].rearrange("p (a q) -> p a q", q=P),
                                      x_t[0][:, :, cols], ALU.subtract).then_inc(ct_lo, 1)
                for j in range(CH):
                    xt = x[:, bass.ds(CH * b + j, 1), :].rearrange("p a n -> p (a n)")
                    dve.wait_ge(o_full, CH * b + j + 1)
                    dve.scalar_tensor_tensor(xt, ps[:, j, :], 1.0 / (CS * WS), xt, ALU.mult, ALU.add)\
                       .then_inc(o_step, 1)
                    dve.wait_ge(o_step, CH * b + j + 1)
                    dve.tensor_tensor(xt, xt, bias_o, ALU.add).then_inc(o_added, 1)
            ffn(1)

        @block.tensor
        def _(pe):
            def mm3(dst, st, mv, first, last):
                pe.matmul(dst, st[0], mv[0], start=first, stop=False)
                pe.matmul(dst, st[0], mv[1], start=False, stop=False)
                return pe.matmul(dst, st[1], mv[0], start=False, stop=last)

            fills = [0]

            def fill(blocks):
                if fills[0] >= 1:
                    pe.wait_ge(tr_lo, fills[0])
                for i, blk in enumerate(blocks):
                    last = pe.transpose(ps[:, TR, i * P:(i + 1) * P], blk, ident[:, :])
                last.then_inc(tr_full, 1)
                fills[0] += 1

            def normed(t):
                pe.wait_ge(xa_norm, t + 1)
                fill([xn_a[:, hb * P:(hb + 1) * P] for hb in range(HB)])

            def project(w, bank, t):
                j = t % 2
                for hb in range(HB):
                    if t == 0:
                        pe.wait_ge(wa_lo, hb + 1 + (HB if bank else 0))
                    for c in range(3):
                        a, e = c * 512, min(IA, (c + 1) * 512)
                        last = mm3(psf[:, bank * 512 + a:bank * 512 + e],
                                   [q[:, hb, j * P:(j + 1) * P] for q in xa_t], [q[:, hb, a:e] for q in w],
                                   hb == 0, hb == HB - 1)
                return last

            def turn(n, j, k):
                w = min(4, AB - k)
                fill([prod[:, n % 2, j, (k + i) * P:(k + i + 1) * P] for i in range(w)])

            def down(n, j):
                t = 2 * n + j
                pe.wait_ge(tr_lo, fills[0])
                if t >= 1:
                    pe.wait_ge(da_added, t)
                for k in range(AB):
                    last = mm3(ps[:, DO, :], [q[:, k, :] for q in ha_t], [q[:, k, :] for q in da],
                               k == 0, k == AB - 1)
                last.then_inc(da_full, 1)

            pe.wait_ge(const_ready, 1)
            for t in range(2):
                normed(t)
            for n in range(PAIRS + 1):
                if n < PAIRS:
                    pe.wait_ge(tr_lo, fills[0])
                    for j in range(2):
                        t = 2 * n + j
                        if t >= 1:
                            pe.wait_ge(ga_silu, t)
                        project(ga, 0, t).then_inc(ga_full, 1)
                        if t >= 1:
                            pe.wait_ge(ua_used, t)
                        project(ua, 3, t).then_inc(ua_full, 1)
                    if n + 1 < PAIRS:
                        for j in range(2):
                            normed(2 * n + 2 + j)
                if n >= 1:
                    if n == 1:
                        pe.wait_ge(pads_zero, 3)
                        pe.wait_ge(wa_lo, 2 * HB + 2)
                    for j in range(2):
                        pe.wait_ge(pruned, 2 * n - 1 + j)
                        for k in range(0, AB, 4):
                            turn(n - 1, j, k)
                        down(n - 1, j)

            def norm(i, xn):
                for j in range(CH):
                    pe.wait_ge(ln_norm, CH * i + j + 1)
                    for hb in range(HB):
                        last = pe.transpose(ps[:, 4 + j, hb * P:(hb + 1) * P], xn[j % 2][:, hb * P:(hb + 1) * P],
                                            ident[:, :])
                    last.then_inc(ln_full, 1)
                pe.wait_ge(ln_lo, CH * i + CH)

            def ffn(f):
                with pe.Fori(0, CHUNKS) as c:
                    m0 = CHUNKS * FB * f + FB * c

                    def gate_up(ib, b, reuse):
                        cols = bass.ds(ib * P, P)
                        for w, bank, full, used in ((fg, 4 + b, gf_full, gf_silu), (fu, 6 + b, uf_full, hf_ready)):
                            if reuse:
                                pe.wait_ge(used, m0 + ib - 1)
                            for hb in range(HB):
                                last = mm3(ps[:, bank, :], [q[:, hb, cols] for q in w], [q[:, hb, :] for q in x_t],
                                           hb == 0, hb == HB - 1)
                            last.then_inc(full, 1)

                    def down(ib, b, first, last):
                        pe.wait_ge(hf_lo, m0 + ib + 1)
                        row = [q[:, bass.ds(ib, 1), :].rearrange("p a n -> p (a n)") for q in fd]
                        for j in range(CH):
                            mm = mm3(ps[:, j, :], [q[:, j * P:(j + 1) * P] for q in h_t[b]], row, first, last)
                        mm.then_inc(df_done, 1)

                    norm(2 * CHUNKS * f + c, xn_f)
                    if f == 0:
                        pe.wait_ge(q_lo, N_GU)
                    gate_up(0, 0, False)
                    gate_up(1, 1, False)
                    if f == 0:
                        pe.wait_ge(q_lo, N_GU + N_D)
                    down(0, 0, True, False)
                    with pe.Fori(1, FB // 2) as k:
                        gate_up(2 * k, 0, True)
                        down(2 * k - 1, 1, False, False)
                        gate_up(2 * k + 1, 1, True)
                        down(2 * k, 0, False, False)
                    down(FB - 1, 1, False, True)

            ffn(0)

            pe.wait_ge(aw_lo, 2)
            pe.wait_ge(df_added, TILES)
            with pe.Fori(0, CHUNKS) as b:
                norm(CHUNKS + b, xn_b)
                for i in range(8):
                    if i >= 4:
                        pe.wait_ge(qk_biased, 8 * b + i - 3)
                    for hb in range(HB):
                        last = mm3(ps[:, i % 4, :], [q[:, hb, i * P:(i + 1) * P] for q in wqkv],
                                   [q[:, hb, :] for q in x_t], hb == 0, hb == HB - 1)
                    last.then_inc(qk_mm, 1)
                for j in range(CH):
                    pe.wait_ge(qk_biased, 8 * b + 5 + j)
                    for hb in range(HB):
                        last = mm3(ps[:, j, :], [q[:, hb, j * P:(j + 1) * P] for q in x_t],
                                   [q[:, hb, 2 * H:3 * H] for q in wqkv], hb == 0, hb == HB - 1)
                    last.then_inc(v_mm, 1)
                pe.wait_ge(v_ready, CH * b + CH)
                pe.wait_ge(v_ones, 2 * b + 2)
                pe.wait_ge(stacked, 768 * b + 768)

                def scores(s, qt):
                    if s < SLOTS:
                        for j in range(2):
                            r = 8 * s + 2 * qt + j
                            if r >= 2:
                                pe.wait_ge(max_done, 8 * SLOTS * b + r - 1)
                            rows = slice(64 * j, 64 * j + 3 * HD)
                            pe.matmul(ps[:, j, :], q_st[rows, s, qt * P:(qt + 1) * P], k_st[rows, s, :],
                                      start=True, stop=True).then_inc(s1_full, 1)

                def turn_maxima(g, slots):
                    if slots:
                        pe.wait_ge(ctx_done, SLOTS * b + slots)
                    pe.wait_ge(max_done, 8 * SLOTS * b + 8 * GS * (g + 1))
                    if g >= 1:
                        pe.wait_ge(mt_ready, GROUPS * b + g)
                    for qt in range(CH):
                        last = pe.transpose(ps[0:2 * GS, 7, qt * P:(qt + 1) * P],
                                            maxima[:, qt, 2 * GS * g:2 * GS * (g + 1)], ident[:, :])
                    last.then_inc(mt_full, 1)

                def scores_t(s, half):
                    if s % GS == 0 and half == 0:
                        pe.wait_ge(max_moved[s // GS], 32 * b + 32)
                    for j in range(2):
                        e = 4 * s + 2 * half + j
                        if e >= 2:
                            pe.wait_ge(exp_done, 4 * SLOTS * b + e - 1)
                    for kk in range(2):
                        for j in range(2):
                            rows = slice(64 * j, 64 * j + 3 * HD + 1)
                            kb = 2 * half + kk
                            mm = pe.matmul(ps[:, 2 + 2 * j + kk, :], k_st[rows, s, kb * P:(kb + 1) * P],
                                           q_st[rows, s, :], start=True, stop=True)
                            if kk == 1:
                                mm.then_inc(s2_full, 1)

                def weigh(s, half):
                    pe.wait_ge(exp_done, 4 * SLOTS * b + 4 * s + 2 * half + 2)
                    if half == 0 and s >= 1:
                        pe.wait_ge(wt_ready, SLOTS * b + s)
                    for j in range(2):
                        for kk in range(2):
                            part = slice(32 * (2 * j + kk), 32 * (2 * j + kk + 1))
                            at, kb = (2 * s + j) * HD1, 2 * half + kk
                            mm = pe.matmul(ps[part, 6, :], v_aug[:, kb, at:at + 32], probs[:, j, kb, :],
                                           start=(half == 0), stop=(half == 1))
                    mm.then_inc(pv_done, 1)

                def turn_weighted(s, turned):
                    pe.wait_ge(wt_ready, SLOTS * b + s + 1)
                    if s >= 1:
                        pe.wait_ge(ctx_done, SLOTS * b + s)
                    if turned:
                        pe.wait_ge(mt_ready, GROUPS * b + turned)
                    for qt in range(CH):
                        mm = pe.transpose(ps[:, 7, qt * P:(qt + 1) * P], weighted_t[:, qt * P:(qt + 1) * P],
                                          ident[:, :])
                    mm.then_inc(w_turned, 1)

                turned = 0
                for u in range(SLOTS + LAG + 1):
                    s = u - LAG
                    scores(u, 0)
                    if 0 <= s < SLOTS:
                        scores_t(s, 0)
                    if u >= GS and u % GS == 0 and u // GS <= GROUPS:
                        turn_maxima(turned, max(0, s - 1))
                        turned += 1
                    scores(u, 1)
                    if s >= 1:
                        weigh(s - 1, 1)
                    scores(u, 2)
                    if 0 <= s < SLOTS:
                        scores_t(s, 1)
                    if s >= 1:
                        turn_weighted(s - 1, turned)
                    scores(u, 3)
                    if 0 <= s < SLOTS:
                        weigh(s, 0)

                pe.wait_ge(ctx_done, SLOTS * b + SLOTS)
                for j in range(CH):
                    for i in range(HB):
                        last = pe.transpose(ps[:, 4 + j, i * P:(i + 1) * P], context[:, i, j, :], ident[:, :])
                    last.then_inc(ct_full, 1)
                for j in range(CH):
                    pe.wait_ge(ct_lo, CH * b + j + 1)
                    for hb in range(HB):
                        last = mm3(ps[:, j, :], [q[:, hb, j * P:(j + 1) * P] for q in x_t],
                                   [q[:, hb, :] for q in wo], hb == 0, hb == HB - 1)
                    last.then_inc(o_full, 1)
            pe.wait_ge(o_added, TILES)
            ffn(1)


def kernel(**inputs):
    import numpy as np
    import concourse.bacc as bacc
    from concourse.bass_utils import run_bass_kernel_spmd

    a = {k.removeprefix("L0_"): np.asarray(v) for k, v in inputs.items()}
    shape = a["attn_a_x"].shape
    laid = {
        "x": a["attn_a_x"].reshape(-1, shape[-1]),
        "w_gate_t": a["attn_a_w_gate"].T, "w_up_t": a["attn_a_w_up"].T, "w_down_t": a["attn_a_w_down"].T,
        "qkvw": a["attn_b_attn_qkvw"], "qkvb": a["attn_b_attn_qkvb"],
        "ow": a["attn_b_attn_ow"], "ob": a["attn_b_attn_ob"],
    }
    for m in ("gate", "up", "down"):
        for part in "wzs":
            laid[f"{m}_{part}"] = a[f"ffn_{m}_{part}"]
    nc = bacc.Bacc("TRN2", target_bir_lowering=False, num_devices=1)
    arrays, args = {}, []
    for name, v in laid.items():
        v = np.ascontiguousarray(v)
        arrays[f"in_{name}"] = v
        args.append(nc.dram_tensor(f"in_{name}", v.shape, mybir.dt.from_np(v.dtype), kind="ExternalInput").ap())
    args.append(nc.dram_tensor("out_x", laid["x"].shape, F32, kind="ExternalOutput").ap())
    hybrid_layers(nc, *args)
    r = run_bass_kernel_spmd(nc, [arrays], core_ids=[0])
    return r.results[0]["out_x"].reshape(shape)
```

```python
from contextlib import ExitStack

import concourse.bass as bass
from concourse import mybir

F32 = mybir.dt.float32
F16 = mybir.dt.float16
I32 = mybir.dt.int32
ALU = mybir.AluOpType
ACT = mybir.ActivationFunctionType
AX = mybir.AxisListType.X

P = 128
EPS = 1e-5
WS = 64.0
HS = 4.0
CS = 8.0
NEWTON = 4
COUNTS = 5
FIRST_LOOKS = 3
GUESS = 0.785
WORK = 17592
SLOPE = 0.0016


class Steps:

    def __init__(self, engine, semaphore):
        self.engine, self.semaphore, self.base, self.n = engine, semaphore, 0, 0

    def did(self, instruction):
        instruction.then_inc(self.semaphore, 1)
        self.n += 1

    def settle(self):
        self.engine.wait_ge(self.semaphore, self.base + self.n)


def hybrid_layers(nc, x_in, w_gate_t, w_up_t, w_down_t, qkvw, qkvb, ow, ob,
                  gate_w, gate_z, gate_s, up_w, up_z, up_s, down_w, down_z, down_s, out):
    TOK, H = x_in.shape
    HB = H // P
    TILES = TOK // P
    IA = w_gate_t.shape[1]
    AB = -(-IA // P)
    AR = IA - (AB - 1) * P
    IAP = AB * P
    K_ZERO = IA // 2
    IF = gate_w.shape[1]
    FB = IF // P
    HEADS, HD = 32, 16
    CH = 4
    CT = CH * P
    CHUNKS = TILES // CH
    PAIRS = TILES // 2
    GB = -(-AB // 4)
    SLOTS = HEADS // 2
    GROUPS = 8
    GS = SLOTS // GROUPS
    LAG = 4
    QK_ORDER = (0, 1, 4, 5, 2, 3, 6, 7)
    CW = 256
    QC = IF // CW
    N_GU = 2 * HB * QC
    N_D = FB * (H // CW)
    HD1 = HD + 1
    assert CHUNKS == 2 and H == 512 and IF % CW == 0 and TILES % CH == 0 and FB % 2 == 0

    ctx = ExitStack()
    with ctx:
        def sb(name, shape, dt):
            return ctx.enter_context(nc.sbuf_tensor(name, shape, dt))

        def sem(name):
            return ctx.enter_context(nc.semaphore(name))

        x = sb("x", [P, TILES, H], F32)
        wa = sb("wa", [P, 4 * HB * IA + 2 * AB * H], F16)
        wf = sb("wf", [P, 4 * HB * IF], F16)
        work = sb("work", [P, WORK + 72], F32)
        ident = sb("ident", [P, P], F32)
        rank8 = sb("rank8", [P, 2, 8], F32)
        bits = sb("bits", [P, 2], I32)
        newton = sb("newton", [P, TILES], F32)
        bias_qk = sb("bias_qk", [P, 8], F32)
        stats = sb("stats", [P, TILES, 6], F32)
        mean_var = sb("mean_var", [P, TILES, 2], F32)
        var_eps = sb("var_eps", [P, TILES], F32)
        rstd = sb("rstd", [P, TILES], F32)
        recip = sb("recip", [P, 2 * CH], F32)
        sums = sb("sums", [P, PAIRS, 2], F32)
        cur = sb("cur", [P, 4], F32)
        signs = sb("signs", [P, 1], F32)
        low = sb("low", [P, 4], F32)
        high = sb("high", [P, 4], F32)
        diff = sb("diff", [P, 4], F32)
        take_low = sb("take_low", [P, 4], I32)
        take_high = sb("take_high", [P, 4], I32)
        frac = sb("frac", [P, 2], F32)
        above = sb("above", [P, 2], F32)
        top8 = sb("top8", [P, 2, 8], F32)
        pick8 = sb("pick8", [P, 8], F32)
        thresh = sb("thresh", [P, 2], F32)
        before = sb("before", [P, 2], F32)
        tied = sb("tied", [P, 4], F32)
        bad = sb("bad", [P, 32], F32)
        bad_t = sb("bad_t", [P, 32], F32)
        bad_q = sb("bad_q", [P, 1], F32)
        bad_row = sb("bad_row", [1, 4], F32)
        bad_flag = sb("bad_flag", [1, 1], I32)

        fold = work[:, WORK:WORK + 64]

        pad = work[:, WORK + 64:WORK + 65]

        def f16(t, at, *dims):
            n = 1
            for d in dims:
                n *= d
            v = t[:, at:at + n]
            if len(dims) == 2:
                return v.rearrange("p (a b) -> p a b", a=dims[0])
            if len(dims) == 3:
                return v.rearrange("p (a b c) -> p a b c", a=dims[0], b=dims[1])
            return v

        work16 = work[:, :].bitcast(F16)
        work32i = work[:, :].bitcast(I32)
        GA = HB * IA
        ga = [f16(wa, 0, HB, IA), f16(wa, GA, HB, IA)]
        ua = [f16(wa, 2 * GA, HB, IA), f16(wa, 3 * GA, HB, IA)]
        da = [f16(wa, 4 * GA, AB, H), f16(wa, 4 * GA + AB * H, AB, H)]
        at = 2 * FB * H
        fd = [f16(wa, 0, FB, H), f16(wa, FB * H, FB, H)]
        wqkv = [f16(wa, at, HB, 3 * H), f16(wa, at + 3 * HB * H, HB, 3 * H)]
        at += 6 * HB * H
        wo = [f16(wa, at, HB, H), f16(wa, at + HB * H, HB, H)]
        at += 2 * HB * H
        bias_v = f16(wa, at, 2 * H).bitcast(F32)
        bias_o = f16(wa, at + 2 * H, 2 * H).bitcast(F32)
        assert 2 * FB * H <= 4 * GA and at + 4 * H <= 4 * GA + 2 * AB * H
        GF = HB * IF
        fg = [f16(wf, 0, HB, IF), f16(wf, GF, HB, IF)]
        fu = [f16(wf, 2 * GF, HB, IF), f16(wf, 3 * GF, HB, IF)]
        FREE = HB * CT + CH * H + 6 * CT
        LAST = FREE + 2 * IA

        def pair_of(at, n):
            return work[:, at:at + 2 * n].rearrange("p (j n) -> p j n", j=2)

        v_abs = [pair_of(0, IA), pair_of(FREE, IA)]
        prod = [pair_of(2 * IA, IAP), pair_of(LAST, IAP)]
        at = 2 * IA + 2 * IAP
        xa_t = [f16(work16, 2 * at, HB, 2 * P), f16(work16, 2 * at + HB * 2 * P, HB, 2 * P)]
        at += HB * 2 * P
        xn_a = work[:, at:at + H]
        assert at + H <= FREE
        at = LAST + 2 * IAP
        scratch = work[:, at:at + IA]
        scratch16 = f16(work16, 2 * at, 2, IA)
        at += IA
        ha_t = [f16(work16, 2 * at, AB, P), f16(work16, 2 * at + AB * P, AB, P)]
        at += AB * P
        quant = work[:, at:at + 6 * CW].rearrange("p (b k n) -> p b k n", b=2, k=3)
        quant_i = work32i[:, at:at + 6 * CW].rearrange("p (b k n) -> p b k n", b=2, k=3)
        assert at + 6 * CW <= WORK
        gate_stage = work[:, 0:GA].rearrange("p (a b) -> p a b", a=HB)
        up_stage = work[:, FREE:FREE + GA].rearrange("p (a b) -> p a b", a=HB)
        DS = 4 * GF - 2 * AB * H
        down_stage = wf[:, DS:4 * GF].bitcast(F32).rearrange("p (a b) -> p a b", a=AB)
        assert GA <= 2 * IA + 2 * IAP and FREE + GA <= LAST + 2 * IAP + IA

        x_t = [f16(work16, 0, HB, CT), f16(work16, HB * CT, HB, CT)]
        at = HB * CT
        xn = [work[:, at + j * H:at + (j + 1) * H] for j in range(CH)]
        at += CH * H
        h_t = [[f16(work16, 2 * at + (2 * b + s) * CT, CT) for s in range(2)] for b in range(2)]
        at += 2 * CT
        silu_f = [work[:, at + b * CT:at + (b + 1) * CT] for b in range(2)]
        at += 2 * CT
        h_f = [work[:, at + b * CT:at + (b + 1) * CT] for b in range(2)]
        at += 2 * CT
        assert at == FREE
        attn_stage = work[:, at:at + 4 * HB * H]
        assert at + 4 * HB * H <= WORK
        context = work[:, 0:HB * CT].rearrange("p (i t d) -> p i t d", i=HB, t=CH)
        at = HB * CT
        q_st = f16(work16, 2 * at, SLOTS, CT)
        at += SLOTS * CT // 2
        k_st = f16(work16, 2 * at, SLOTS, CT)
        at += SLOTS * CT // 2
        VW = HEADS * HD1 + 32 - HD1
        v_aug = work[:, at:at + CH * VW].rearrange("p (t n) -> p t n", t=CH)
        v_heads = v_aug[:, :, 0:HEADS * HD1].rearrange("p t (h d) -> p t h d", h=HEADS)
        qk_full = [work[:, at + b * H:at + (b + 1) * H] for b in range(2)]
        at += CH * VW
        probs = work[:, at:at + 2 * CH * CT].rearrange("p (j k n) -> p j k n", j=2, k=CH)
        qk_part = f16(work16, 2 * at, 8, 2, CT)
        at += 2 * CH * CT
        maxima = work[:, at:at + CH * HEADS].rearrange("p (t h) -> p t h", t=CH)
        at += CH * HEADS
        max_rows = f16(work16, 2 * at, CT)
        at += CT // 2
        weighted_t = work[:, at:at + CT]
        at += CT
        assert at <= WORK

        ps = ctx.enter_context(nc.psum_tensor("ps", [P, 8, 512], F32))
        psf = ps[:, :, :].rearrange("p b n -> p (b n)")
        TR, DO = 6, 7

        x_loaded = [sem(f"x_loaded{i}") for i in range(2)]
        wg_loaded = [sem(f"wg_loaded{i}") for i in range(HB)]
        wu_loaded = [sem(f"wu_loaded{i}") for i in range(HB)]
        wd_loaded, bias_loaded = sem("wd_loaded"), sem("bias_loaded")
        attn_w_loaded = sem("attn_w_loaded")
        q_loaded = [sem(f"q_loaded{i}") for i in range(2)]
        const_step, const_ready, fold_ready = sem("const_step"), sem("const_ready"), sem("fold_ready")
        wa_hi, wa_lo = sem("wa_hi"), sem("wa_lo")
        q_sub, q_float, q_mul, q_hi, q_lo = (sem(n) for n in ("q_sub", "q_float", "q_mul", "q_hi", "q_lo"))
        aw_scaled, aw_hi, aw_lo = sem("aw_scaled"), sem("aw_hi"), sem("aw_lo")
        pads_zero = sem("pads_zero")
        xa_norm, tr_full, tr_hi, tr_lo = sem("xa_norm"), sem("tr_full"), sem("tr_hi"), sem("tr_lo")
        ga_full, ga_silu, ga_abs = sem("ga_full"), sem("ga_silu"), sem("ga_abs")
        ua_full, ua_used = sem("ua_full"), sem("ua_used")
        pruned, da_full, da_added = sem("pruned"), sem("da_full"), sem("da_added")
        cut_ready, cut_counted = sem("cut_ready"), sem("cut_counted")
        sel_step, fallback_step = sem("sel_step"), sem("fallback_step")
        ln_step = sem("ln_step")
        ln_norm, ln_full, ln_hi, ln_lo = sem("ln_norm"), sem("ln_full"), sem("ln_hi"), sem("ln_lo")
        gf_full, gf_silu, uf_full, hf_ready = sem("gf_full"), sem("gf_silu"), sem("uf_full"), sem("hf_ready")
        hf_hi, hf_lo, df_done, df_added = sem("hf_hi"), sem("hf_lo"), sem("df_done"), sem("df_added")
        qk_mm, qk_biased, qk_hi, qk_lo = sem("qk_mm"), sem("qk_biased"), sem("qk_hi"), sem("qk_lo")
        stacked, stacked_pool = ([sem(f"{n}{i}") for i in range(2)] for n in ("stacked", "stacked_pool"))
        ones_row, pad_step = sem("ones_row"), sem("pad_step")
        v_mm, v_ready, v_ones = sem("v_mm"), sem("v_ready"), sem("v_ones")
        s1_full, max_done, mt_full, mt_ready = sem("s1_full"), sem("max_done"), sem("mt_full"), sem("mt_ready")
        max_moved = [sem(f"max_moved{g}") for g in range(GROUPS)]
        s2_full, exp_done, pv_done = sem("s2_full"), sem("exp_done"), sem("pv_done")
        wt_ready, w_turned, ctx_step, ctx_done = sem("wt_ready"), sem("w_turned"), sem("ctx_step"), sem("ctx_done")
        ct_full, ct_hi, ct_lo, o_full = sem("ct_full"), sem("ct_hi"), sem("ct_lo"), sem("o_full")
        o_step, o_added = sem("o_step"), sem("o_added")
        stored = sem("stored")

        block = ctx.enter_context(nc.Block())

        def quant_chunk(c):
            if c < N_GU:
                m, hb, k = c // (HB * QC), c // QC % HB, c % QC
                w, z, s = ((gate_w, gate_z, gate_s), (up_w, up_z, up_s))[m]
                dst = (fg, fu)[m]
            else:
                hb, k = (c - N_GU) // (H // CW), (c - N_GU) % (H // CW)
                w, z, s, dst = down_w, down_z, down_s, fd
            cols = slice(k * CW, (k + 1) * CW)
            return (w[hb * P:(hb + 1) * P, cols], z[hb:hb + 1, cols].to_broadcast([P, CW]),
                    s[hb:hb + 1, cols].to_broadcast([P, CW]), dst[0][:, hb, cols], dst[1][:, hb, cols])

        def stack_parts(engine, b, places, done, carrier=None):
            for h in range(2):
                for m, (stack, parts) in enumerate(((q_st, (0, 0, 1)), (k_st, (0, 1, 0)))):
                    engine.wait_ge(qk_lo, 8 * b + 4 * h + 2 * m + 2)
                    if m == 1:
                        engine.wait_ge(ones_row, 1)
                    if carrier is not None:
                        carrier(2 * h + m)
                    blocks = slice(4 * m + 2 * h, 4 * m + 2 * h + 2)
                    for r in places:
                        for j in range(2):
                            for pp in range(4):
                                src, slots = (2 * pp + j) * HD, slice(8 * h + pp, 8 * h + 8, 4)
                                engine.dma_start(stack[64 * j + HD * r:64 * j + HD * (r + 1), slots, :],
                                                 qk_part[src:src + HD, blocks, parts[r], :]).then_inc(done[h], 16)

        @block.sync
        def _(sp):
            xr = x_in.rearrange("(t p) h -> p t h", p=P)
            sp.dma_start(x[:, 0:2, :], xr[:, 0:2, :]).then_inc(x_loaded[0], 16)
            for hb in range(HB):
                sp.dma_start(gate_stage[:, hb, :], w_gate_t[hb * P:(hb + 1) * P, :]).then_inc(wg_loaded[hb], 16)
            for hb in range(HB):
                sp.dma_start(up_stage[:, hb, :], w_up_t[hb * P:(hb + 1) * P, :]).then_inc(wu_loaded[hb], 16)
            sp.dma_start(x[:, 2:TILES, :], xr[:, 2:TILES, :]).then_inc(x_loaded[1], 16)
            full = (AB - 1) * P
            sp.dma_start(down_stage[:, 0:AB - 1, :],
                         w_down_t[0:full, :].rearrange("(a p) n -> p a n", p=P)).then_inc(wd_loaded, 16)
            sp.dma_start(down_stage[0:AR, AB - 1, :], w_down_t[full:IA, :]).then_inc(wd_loaded, 16)
            with nc.allow_non_contiguous_dma(reason="8 bias values of a partition"):
                sp.dma_start(bias_qk[:, :], qkvb[0:2 * H].rearrange("(i p) -> p i", p=P)).then_inc(bias_loaded, 16)
            for c in range(N_GU + N_D):
                w, z, s, _, _ = quant_chunk(c)
                b = c % 2
                if c >= 2:
                    sp.wait_ge(q_sub, c - 1)
                sp.dma_start(quant_i[:, b, 1, :], z).then_inc(q_loaded[b], 16)
                if c >= 2:
                    sp.wait_ge(q_mul, c - 1)
                sp.dma_start(quant_i[:, b, 0, :], w).then_inc(q_loaded[b], 16)
                if c >= 2:
                    sp.wait_ge(q_lo, c - 1)
                sp.dma_start(quant[:, b, 2, :], s).then_inc(q_loaded[b], 16)
            sp.wait_ge(da_added, TILES)
            st = attn_stage.rearrange("p (a n) -> p a n", a=HB)
            sp.dma_start(st[:, :, 0:3 * H], qkvw.rearrange("(a p) n -> p a n", p=P)).then_inc(attn_w_loaded, 16)
            sp.dma_start(st[:, :, 3 * H:4 * H], ow.rearrange("(a p) n -> p a n", p=P)).then_inc(attn_w_loaded, 16)
            sp.dma_start(bias_v, qkvb[2 * H:3 * H].rearrange("(a n) -> a n", a=1).to_broadcast([P, H]))\
              .then_inc(attn_w_loaded, 16)
            sp.dma_start(bias_o, ob.rearrange("(a n) -> a n", a=1).to_broadcast([P, H])).then_inc(attn_w_loaded, 16)

            with sp.Fori(0, CHUNKS) as b:
                stack_parts(sp, b, (0, 1), stacked)

            outr = out.rearrange("(t p) h -> p t h", p=P)
            for t in range(TILES):
                sp.wait_ge(df_added, TILES + t + 1)
                sp.dma_start(outr[:, t, :], x[:, t, :]).then_inc(stored, 16)
            sp.wait_ge(stored, 16 * TILES)

        @block.gpsimd
        def _(pool):
            pool.memset(ident[:, :], 0.0).then_inc(const_step, 1)
            pool.wait_ge(const_step, 1)
            pool.affine_select(out=ident[:, :], in_=ident[:, :], compare_op=ALU.not_equal, fill=1.0, base=0,
                               pattern=[[-1, P]], channel_multiplier=1).then_inc(const_ready, 1)
            pool.wait_ge(const_ready, 1)
            halves = ident[:, :].rearrange("p (j k d) -> p j k d", j=2, k=2)
            pool.tensor_tensor(fold.rearrange("p (j d) -> p j d", j=2), halves[:, :, 0, :], halves[:, :, 1, :],
                               ALU.add).then_inc(fold_ready, 1)
            pool.iota(rank8[:, :, :], pattern=[[1, 2], [1, 8]], base=0, channel_multiplier=0,
                      allow_small_or_imprecise_dtypes=True).then_inc(const_ready, 1)
            pool.memset(bad[:, :], 0.0).then_inc(const_ready, 1)

            for c in range(N_GU + N_D):
                b = c % 2
                _, _, _, hi, lo = quant_chunk(c)
                value_i, value, product = quant_i[:, b, 0, :], quant[:, b, 0, :], quant[:, b, 2, :]
                pool.wait_ge(q_loaded[b], 48 * (c // 2 + 1))
                pool.tensor_tensor(value_i, value_i, quant_i[:, b, 1, :], ALU.subtract).then_inc(q_sub, 1)
                pool.wait_ge(q_sub, c + 1)
                pool.tensor_scalar(value, value_i, WS, 0.0, ALU.mult, ALU.add).then_inc(q_float, 1)
                pool.wait_ge(q_float, c + 1)
                pool.tensor_tensor(product, value, product, ALU.mult).then_inc(q_mul, 1)
                if c == HB * QC:
                    pool.wait_ge(wa_lo, 2 * HB + 2)
                if c == N_GU:
                    pool.wait_ge(ga_full, TILES)
                    pool.wait_ge(ua_full, TILES)
                pool.wait_ge(q_mul, c + 1)
                pool.tensor_scalar(hi, product, 1.0, 0.0, ALU.mult, ALU.add).then_inc(q_hi, 1)
                pool.wait_ge(q_hi, c + 1)
                pool.tensor_tensor(lo, product, hi, ALU.subtract).then_inc(q_lo, 1)

            pool.wait_ge(attn_w_loaded, 64)
            st = attn_stage.rearrange("p (a n) -> p a n", a=HB)
            for i, (cols, dst) in enumerate(((slice(0, 3 * H), wqkv), (slice(3 * H, 4 * H), wo))):
                pool.tensor_scalar(st[:, :, cols], st[:, :, cols], WS, 0.0, ALU.mult, ALU.add).then_inc(aw_scaled, 1)
                pool.wait_ge(aw_scaled, i + 1)
                pool.tensor_copy(dst[0], st[:, :, cols]).then_inc(aw_hi, 1)
                pool.wait_ge(aw_hi, i + 1)
                pool.tensor_tensor(dst[1], st[:, :, cols], dst[0], ALU.subtract).then_inc(aw_lo, 1)
            pool.wait_ge(df_added, TILES)
            pool.wait_ge(aw_lo, 2)
            pool.memset(k_st, 1.0).then_inc(ones_row, 1)
            pool.memset(pad, 0.0).then_inc(pad_step, 1)
            with pool.Fori(0, CHUNKS) as b:
                def carrier(k):
                    pool.wait_ge(pad_step, (4 + GROUPS) * b + k + 1)
                    pool.tensor_tensor(pad, pad, pad, ALU.subtract).then_inc(pad_step, 1)

                stack_parts(pool, b, (2,), stacked_pool, carrier)
                for g in range(GROUPS):
                    pool.wait_ge(mt_ready, GROUPS * b + g + 1)
                    carrier(4 + g)
                    for j in range(2):
                        pool.dma_start(q_st[64 * j + 48:64 * j + 49, GS * g:GS * (g + 1), :],
                                       max_rows[j:2 * GS:2, :]).then_inc(max_moved[g], 16)

        @block.scalar
        def _(act):
            fills = [0]

            def fill(parts, width, bank=TR):
                act.wait_ge(tr_full, fills[0] + 1)
                act.activation(parts, psf[:, bank * 512:bank * 512 + width].rearrange("p (a q) -> p a q", q=P),
                               ACT.Copy).then_inc(tr_hi, 1)
                fills[0] += 1

            def fill_x(t):
                fill(xa_t[0][:, :, t % 2 * P:(t % 2 + 1) * P], H)

            def fill_h(g, bank):
                w = min(4, AB - 4 * g)
                fill(ha_t[0][:, 4 * g:4 * g + w, :], w * P, bank)

            def count(n, it):
                act.wait_ge(cut_ready, COUNTS * n + it + 1)
                act.activation(scratch16[:, 1, :], v_abs[n % 2][:, 1, :], ACT.Sign, scale=-1.0, bias=cur[:, 1:2],
                               accum_out=signs[:, :]).then_inc(cut_counted, 1)

            for t in range(2):
                fill_x(t)
            for loaded, stage, dst in ((wg_loaded, gate_stage, ga), (wu_loaded, up_stage, ua)):
                for hb in range(HB):
                    act.wait_ge(loaded[hb], 16)
                    act.activation(dst[0][:, hb, :], stage[:, hb, :], ACT.Copy, scale=WS).then_inc(wa_hi, 1)
            act.wait_ge(wd_loaded, 32)
            act.activation(da[0][:, 0:AB - 1, :], down_stage[:, 0:AB - 1, :], ACT.Copy, scale=WS).then_inc(wa_hi, 1)
            act.activation(da[0][0:AR, AB - 1, :], down_stage[0:AR, AB - 1, :], ACT.Copy, scale=WS).then_inc(wa_hi, 1)
            for n in range(PAIRS):
                if n >= 1:
                    for it in range(FIRST_LOOKS):
                        count(n - 1, it)
                for j in range(2):
                    t = 2 * n + j
                    act.wait_ge(ga_full, t + 1)
                    if t >= 4:
                        act.wait_ge(da_full, t - 3)
                    if n == 0:
                        act.wait_ge(wa_lo, 2 * HB)
                    act.activation(prod[n % 2][:, j, 0:IA], psf[:, 0:IA], ACT.Silu, scale=1.0 / WS)\
                        .then_inc(ga_silu, 1)
                    act.wait_ge(ga_silu, t + 1)
                    if n >= 2:
                        act.wait_ge(pruned, t - 3)
                    act.activation(v_abs[n % 2][:, j, :], prod[n % 2][:, j, 0:IA], ACT.Abs,
                                   accum_out=sums[:, n, j:j + 1]).then_inc(ga_abs, 1)
                    if n + 1 < PAIRS:
                        fill_x(t + 2)
                    if n >= 1 and j == 0:
                        for it in range(FIRST_LOOKS, COUNTS):
                            count(n - 1, it)
                if n >= 1:
                    for j in range(2):
                        for g in range(GB):
                            fill_h(g, g)

            def norm(i):
                for j in range(CH):
                    act.wait_ge(ln_full, CH * i + j + 1)
                    act.activation(x_t[0][:, :, j * P:(j + 1) * P],
                                   ps[:, 4 + j, :].rearrange("p (a q) -> p a q", q=P), ACT.Copy).then_inc(ln_hi, 1)

            def ffn_block(m, b):
                act.wait_ge(gf_full, m + 1)
                act.activation(silu_f[b], ps[:, 4 + b, :], ACT.Silu, scale=1.0 / WS).then_inc(gf_silu, 1)
                act.wait_ge(hf_ready, m + 1)
                act.activation(h_t[b][0], h_f[b], ACT.Copy).then_inc(hf_hi, 1)

            def ffn_chunk(f, c):
                norm(2 * CHUNKS * f + c)
                with act.Fori(0, FB // 2) as k:
                    for b in range(2):
                        ffn_block((CHUNKS * FB * f + FB * c) + 2 * k + b, b)

            norm(0)
            for ib in range(FB):
                ffn_block(ib, ib % 2)
                if ib < COUNTS:
                    count(PAIRS - 1, ib)
            for j in range(2):
                for g in range(GB):
                    fill_h(g, 4 + g)
            ffn_chunk(0, 1)
            with act.Fori(0, CHUNKS) as b:
                norm(CHUNKS + b)
                for n, i in enumerate(QK_ORDER):
                    act.wait_ge(qk_biased, 8 * b + n + 1)
                    act.activation(qk_part[:, i, 0, :], qk_full[n % 2], ACT.Copy).then_inc(qk_hi, 1)

                def exps(s, half):
                    for j in range(2):
                        act.wait_ge(s2_full, 4 * SLOTS * b + 4 * s + 2 * half + j + 1)
                        if s == 0:
                            for h in range(2):
                                act.wait_ge(stacked[h], 512 * b + 512)
                                act.wait_ge(stacked_pool[h], 256 * b + 256)
                        else:
                            act.wait_ge(pv_done, 2 * SLOTS * b + 2 * (s - 1) + half + 1)
                        act.activation(probs[:, j, 2 * half:2 * half + 2, :],
                                       ps[:, 2 + 2 * j:4 + 2 * j, :], ACT.Exp, scale=HD ** -0.5).then_inc(exp_done, 1)

                def rows(g):
                    act.wait_ge(mt_full, GROUPS * b + g + 1)
                    if g >= 1:
                        act.wait_ge(max_moved[g - 1], 32 * b + 32)
                    act.activation(max_rows[0:2 * GS, :], ps[0:2 * GS, 7, :], ACT.Copy, scale=-1.0)\
                        .then_inc(mt_ready, 1)

                def summed(s):
                    act.wait_ge(pv_done, 2 * SLOTS * b + 2 * s + 2)
                    if s >= 1:
                        act.wait_ge(w_turned, SLOTS * b + s)
                    act.activation(weighted_t, ps[:, 6, :], ACT.Copy).then_inc(wt_ready, 1)

                for u in range(SLOTS + LAG + 1):
                    s = u - LAG
                    if 0 <= s < SLOTS:
                        exps(s, 0)
                    if u >= GS and u % GS == 0 and u // GS <= GROUPS:
                        rows(u // GS - 1)
                    if s >= 1:
                        summed(s - 1)
                    if 0 <= s < SLOTS:
                        exps(s, 1)
                for j in range(CH):
                    act.wait_ge(ct_full, CH * b + CH)
                    act.activation(x_t[0][:, :, j * P:(j + 1) * P],
                                   ps[:, 4 + j, :].rearrange("p (a q) -> p a q", q=P), ACT.Copy).then_inc(ct_hi, 1)
            with act.Fori(0, CHUNKS) as c:
                ffn_chunk(1, c)

        @block.vector
        def _(dve):
            sel = Steps(dve, sel_step)

            def inverse_root(st, lo, hi):
                v, y, a = var_eps[:, lo:hi], rstd[:, lo:hi], newton[:, lo:hi]
                st.did(dve.tensor_scalar(a.bitcast(I32), v.bitcast(I32), 1, None, ALU.logical_shift_right))
                st.settle()
                st.did(dve.tensor_scalar(y.bitcast(I32), a.bitcast(I32), -1.0, float(0x5F3759DF), ALU.mult, ALU.add))
                st.settle()
                for _ in range(NEWTON):
                    st.did(dve.scalar_tensor_tensor(a, y, -0.5, y, ALU.mult, ALU.mult))
                    st.settle()
                    st.did(dve.tensor_tensor(a, a, v, ALU.mult))
                    st.settle()
                    st.did(dve.scalar_tensor_tensor(y, a, 1.5, y, ALU.add, ALU.mult))
                    st.settle()

            def statistics(lo, hi):
                for t in range(lo, hi):
                    sel.did(dve.bn_stats(stats[:, t, :], x[:, t, :]))
                sel.settle()
                for t in range(lo, hi):
                    sel.did(dve.bn_aggr(mean_var[:, t, :], stats[:, t, :]))
                sel.settle()
                sel.did(dve.tensor_scalar(var_eps[:, lo:hi], mean_var[:, lo:hi, 1], EPS, None, ALU.add))
                sel.settle()
                inverse_root(sel, lo, hi)

            dve.wait_ge(x_loaded[0], 16)
            statistics(0, 2)
            def normed(t):
                if t % TILES >= 1:
                    dve.wait_ge(tr_full, x_fill(t - 1) + 1)
                dve.tensor_scalar(xn_a, x[:, t, :], mean_var[:, t, 0:1], rstd[:, t:t + 1],
                                  ALU.subtract, ALU.mult).then_inc(xa_norm, 1)

            def x_fill(t):
                return t if t < 6 else t + 6 * (t // 2 - 2)

            fills = [0]

            def fill(parts, width, bank=TR):
                dve.wait_ge(tr_hi, fills[0] + 1)
                dve.tensor_tensor(parts[1], psf[:, bank * 512:bank * 512 + width].rearrange("p (a q) -> p a q", q=P),
                                  parts[0], ALU.subtract).then_inc(tr_lo, 1)
                fills[0] += 1

            def fill_x(t):
                fill([q[:, :, t % 2 * P:(t % 2 + 1) * P] for q in xa_t], H)

            def fill_h(g, bank):
                w = min(4, AB - 4 * g)
                fill([q[:, 4 * g:4 * g + w, :] for q in ha_t], w * P, bank)

            for t in range(2):
                normed(t)
                fill_x(t)
            for i, (stage, dst) in enumerate(((gate_stage, ga), (up_stage, ua))):
                for hb in range(HB):
                    dve.wait_ge(wa_hi, HB * i + hb + 1)
                    dve.scalar_tensor_tensor(dst[1][:, hb, :], stage[:, hb, :], WS, dst[0][:, hb, :],
                                             ALU.mult, ALU.subtract).then_inc(wa_lo, 1)
            dve.wait_ge(x_loaded[1], 16)
            statistics(2, TILES)
            dve.wait_ge(wa_hi, 2 * HB + 2)
            dve.scalar_tensor_tensor(da[1][:, 0:AB - 1, :], down_stage[:, 0:AB - 1, :], WS, da[0][:, 0:AB - 1, :],
                                     ALU.mult, ALU.subtract).then_inc(wa_lo, 1)
            dve.scalar_tensor_tensor(da[1][0:AR, AB - 1, :], down_stage[0:AR, AB - 1, :], WS, da[0][0:AR, AB - 1, :],
                                     ALU.mult, ALU.subtract).then_inc(wa_lo, 1)
            dve.memset(da[0][AR:P, AB - 1, :], 0.0).then_inc(pads_zero, 1)
            dve.memset(da[1][AR:P, AB - 1, :], 0.0).then_inc(pads_zero, 1)
            dve.wait_ge(wa_lo, 2 * HB)
            for buf in prod:
                dve.memset(buf[:, :, IA:IAP], 0.0).then_inc(pads_zero, 1)

            dve.wait_ge(const_ready, 3)
            GOAL = K_ZERO + 3.5

            def twice(v):
                return v.unsqueeze(1).to_broadcast([P, 2, 2])

            def pairs(v):
                return v.rearrange("p (a b) -> p a b", a=2)

            def count(n, it):
                dve.wait_ge(cut_ready, COUNTS * n + it + 1)
                sel.did(dve.tensor_scalar(scratch16[:, 0, :], v_abs[n % 2][:, 0, :], cur[:, 0:1], None,
                                          ALU.is_le, ALU.add, accum_out=cur[:, 2:3]))
                dve.wait_ge(cut_counted, COUNTS * n + it + 1)
                sel.did(dve.tensor_scalar(cur[:, 3:4], signs[:, :], 0.5, IA / 2, ALU.mult, ALU.add))
                sel.settle()
                sel.did(dve.tensor_scalar(pairs(take_low[:, :]), twice(cur[:, 2:4]), GOAL, None, ALU.is_lt))
                sel.did(dve.tensor_scalar(pairs(take_high[:, :]), twice(cur[:, 2:4]), GOAL, None, ALU.is_gt))
                sel.settle()
                sel.did(dve.copy_predicated(low[:, :], take_low[:, :], cur[:, :]))
                sel.did(dve.copy_predicated(high[:, :], take_high[:, :], cur[:, :]))
                sel.settle()

            def guess(n, it):
                if it == 0:
                    sel.did(dve.tensor_scalar(frac[:, :], cur[:, 2:4], -SLOPE / IA, SLOPE / IA * GOAL,
                                              ALU.mult, ALU.add))
                    sel.settle()
                    sel.did(dve.tensor_tensor(frac[:, :], frac[:, :], sums[:, n, :], ALU.mult))
                    sel.settle()
                    dve.tensor_tensor(cur[:, 0:2], cur[:, 0:2], frac[:, :], ALU.add).then_inc(cut_ready, 1)
                    return
                sel.did(dve.tensor_tensor(diff[:, :], high[:, :], low[:, :], ALU.subtract))
                sel.did(dve.tensor_scalar(frac[:, :], low[:, 2:4], -1.0, GOAL, ALU.mult, ALU.add))
                sel.settle()
                sel.did(dve.reciprocal(above[:, :], diff[:, 2:4]))
                sel.settle()
                sel.did(dve.tensor_tensor(frac[:, :], frac[:, :], above[:, :], ALU.mult))
                sel.settle()
                sel.did(dve.tensor_tensor(frac[:, :], frac[:, :], diff[:, 0:2], ALU.mult))
                sel.settle()
                dve.tensor_tensor(cur[:, 0:2], low[:, 0:2], frac[:, :], ALU.add).then_inc(cut_ready, 1)

            def start(n):
                dve.wait_ge(ga_abs, 2 * n + 2)
                sel.did(dve.memset(low[:, :], 0.0))
                sel.did(dve.tensor_scalar(high[:, 0:2], sums[:, n, :], 8.0 / IA, None, ALU.mult))
                sel.did(dve.memset(high[:, 2:4], float(IA)))
                dve.tensor_scalar(cur[:, 0:2], sums[:, n, :], GUESS / IA, None, ALU.mult).then_inc(cut_ready, 1)
                sel.settle()

            def general(n):
                done = Steps(dve, fallback_step)
                for j in range(2):
                    v = v_abs[n % 2][:, j, :]
                    p = prod[n % 2][:, j, 0:IA]
                    bit, trial = bits[:, 0:1], bits[:, 1:2]
                    found = low[:, j:j + 1]
                    done.did(dve.memset(bit, 1 << 30))
                    done.did(dve.memset(found.bitcast(I32), 0))
                    done.settle()
                    with dve.Fori(0, 31) as i:
                        inner = Steps(dve, fallback_step)
                        inner.base = done.n + 5 * i
                        inner.did(dve.tensor_tensor(trial, found.bitcast(I32), bit, ALU.bitwise_or))
                        inner.settle()
                        inner.did(dve.tensor_scalar(scratch16[:, 0, :], v, trial.bitcast(F32), None, ALU.is_lt, ALU.add,
                                                    accum_out=frac[:, 0:1]))
                        inner.settle()
                        inner.did(dve.tensor_scalar(take_low[:, 0:1], frac[:, 0:1], float(K_ZERO), None, ALU.is_lt))
                        inner.settle()
                        inner.did(dve.tensor_scalar(bit, bit, 1, None, ALU.logical_shift_right))
                        inner.did(dve.copy_predicated(found, take_low[:, 0:1], trial.bitcast(F32)))
                        inner.settle()
                    done.n += 5 * 31
                    done.did(dve.tensor_scalar(scratch16[:, 0, :], v, found, None, ALU.is_lt, ALU.add,
                                               accum_out=frac[:, 0:1]))
                    done.did(dve.tensor_scalar(diff[:, 0:1], found, 1.0, None, ALU.mult))
                    done.settle()
                    done.did(dve.tensor_scalar(frac[:, 0:1], frac[:, 0:1], -1.0, float(K_ZERO), ALU.mult, ALU.add))
                    done.did(dve.tensor_scalar(scratch, v, found, None, ALU.is_equal))
                    done.settle()
                    done.did(dve.tensor_tensor_scan(scratch, scratch, scratch, 0.0, ALU.add, ALU.max))
                    done.settle()
                    done.did(dve.tensor_scalar(scratch, scratch, frac[:, 0:1], None, ALU.is_le))
                    done.settle()
                    done.did(dve.scalar_tensor_tensor(scratch, v, found, scratch, ALU.is_equal, ALU.mult))
                    done.settle()
                    done.did(dve.scalar_tensor_tensor(scratch, v, found, scratch, ALU.is_lt, ALU.add))
                    done.settle()
                    done.did(dve.tensor_scalar(scratch, scratch, -1.0, 1.0, ALU.mult, ALU.add))
                    done.settle()
                    done.did(dve.tensor_tensor(p, p, scratch, ALU.mult))
                    done.did(dve.memset(thresh[:, j:j + 1], -1.0))
                    done.settle()
                dve.sem_clear(fallback_step)

            def finish(n):
                sel.did(dve.tensor_scalar(pairs(take_high[:, :]), twice(high[:, 2:4]), K_ZERO + 7.5, None, ALU.is_lt))
                sel.settle()
                sel.did(dve.copy_predicated(low[:, :], take_high[:, :], high[:, :]))
                sel.settle()
                sel.did(dve.tensor_scalar(above[:, :], low[:, 2:4], -float(K_ZERO), None, ALU.add))
                for j in range(2):
                    v = v_abs[n % 2][:, j, :]
                    sel.did(dve.scalar_tensor_tensor(scratch, v, low[:, j:j + 1], v, ALU.is_le, ALU.mult))
                    sel.settle()
                    sel.did(dve.max(top8[:, j, :], scratch))
                    sel.settle()
                    for k, kept in enumerate((thresh, before)):
                        sel.did(dve.scalar_tensor_tensor(pick8[:, :], rank8[:, k, :], above[:, j:j + 1], top8[:, j, :],
                                                         ALU.is_equal, ALU.mult, accum_out=kept[:, j:j + 1]))
                        sel.settle()

            def verify(n):
                sel.did(dve.tensor_tensor(tied[:, 0:2], thresh[:, :], before[:, :], ALU.is_equal))
                sel.did(dve.tensor_tensor(tied[:, 2:4], top8[:, :, 0], low[:, 0:2], ALU.is_equal))
                sel.settle()
                sel.did(dve.tensor_reduce(bad[:, 0:1], tied[:, :], AX, ALU.max))
                sel.settle()
                sel.did(dve.transpose(bad_t[:, :], bad[:, :]))
                sel.settle()
                sel.did(dve.tensor_reduce(bad_q[:, :], bad_t[:, :], AX, ALU.max))
                sel.settle()
                for q in range(4):
                    sel.did(dve.tensor_copy(bad_row[:, q:q + 1], bad_q[32 * q:32 * q + 1, :]))
                sel.settle()
                sel.did(dve.tensor_reduce(bad_flag[:, :], bad_row[:, :], AX, ALU.max))
                sel.settle()
                failed = dve.value_load(bad_flag[0:1, 0:1])
                with dve.If(failed):
                    general(n)

            def look(n, it):
                if it == 0:
                    start(n)
                count(n, it)
                if it + 1 < COUNTS:
                    guess(n, it)

            def prune(t):
                n, j = t // 2, t % 2
                p = prod[n % 2][:, j, 0:IA]
                dve.wait_ge(ua_used, t + 1)
                dve.scalar_tensor_tensor(p, v_abs[n % 2][:, j, :], thresh[:, j:j + 1], p, ALU.is_gt, ALU.mult)\
                    .then_inc(pruned, 1)

            def product(t):
                n, j = t // 2, t % 2
                p = prod[n % 2][:, j, 0:IA]
                dve.wait_ge(ua_full, t + 1)
                dve.wait_ge(ga_abs, t + 1)
                dve.scalar_tensor_tensor(p, psf[:, 3 * 512:3 * 512 + IA], HS / WS, p, ALU.mult, ALU.mult)\
                    .then_inc(ua_used, 1)

            def ln_stats(st, c, tiles):
                for j in tiles:
                    st.did(dve.bn_stats(stats[:, j, :], x[:, bass.ds(CH * c + j, 1), :].rearrange("p a n -> p (a n)")))
                st.settle()

            def ln_rstd(st, lo, hi):
                dve.memset(newton[:, lo:hi], 0.0)
                for j in range(lo, hi):
                    st.did(dve.bn_aggr(mean_var[:, j, :], stats[:, j, :]))
                st.settle()
                st.did(dve.tensor_scalar(var_eps[:, lo:hi], mean_var[:, lo:hi, 1], EPS, None, ALU.add))
                st.settle()
                inverse_root(st, lo, hi)

            def ln_normed(c, tiles):
                for j in tiles:
                    dve.tensor_scalar(xn[j], x[:, bass.ds(CH * c + j, 1), :].rearrange("p a n -> p (a n)"),
                                      mean_var[:, j, 0:1], rstd[:, j:j + 1], ALU.subtract, ALU.mult)\
                       .then_inc(ln_norm, 1)

            def ln_steps(i):
                st = Steps(dve, ln_step)
                st.base = (2 * CH + 3 + 3 * NEWTON) * (i - CHUNKS)
                return st

            def ln_low(i):
                for j in range(CH):
                    cols = slice(j * P, (j + 1) * P)
                    dve.wait_ge(ln_hi, CH * i + j + 1)
                    dve.tensor_tensor(x_t[1][:, :, cols], ps[:, 4 + j, :].rearrange("p (a q) -> p a q", q=P),
                                      x_t[0][:, :, cols], ALU.subtract).then_inc(ln_lo, 1)

            def down_added(t, bank):
                dve.wait_ge(da_full, t + 1)
                dve.scalar_tensor_tensor(x[:, t, :], ps[:, bank, :], 1.0 / (HS * WS), x[:, t, :],
                                         ALU.mult, ALU.add).then_inc(da_added, 1)

            for n in range(PAIRS):
                t = 2 * n
                if n >= 1:
                    for it in range(FIRST_LOOKS):
                        look(n - 1, it)
                if n + 1 < PAIRS:
                    normed(t + 2)
                product(t)
                if n + 1 < PAIRS:
                    fill_x(t + 2)
                if n >= 1:
                    for it in range(FIRST_LOOKS, COUNTS):
                        look(n - 1, it)
                    finish(n - 1)
                    verify(n - 1)
                    prune(t - 2)
                    prune(t - 1)
                if n + 1 < PAIRS:
                    normed(t + 3)
                product(t + 1)
                if n + 1 < PAIRS:
                    fill_x(t + 3)
                else:
                    ln_stats(sel, 0, range(CH))
                    ln_rstd(sel, 0, CH)
                if n >= 1:
                    for g in range(GB):
                        fill_h(g, g)
                    for g in range(GB):
                        fill_h(g, g)
                        if g == GB - 2:
                            down_added(t - 2, DO)
                    if n + 1 == PAIRS:
                        ln_normed(0, range(CH))
                    down_added(t - 1, TR)

            def ffn_product(m, b):
                dve.wait_ge(uf_full, m + 1)
                dve.wait_ge(gf_silu, m + 1)
                dve.scalar_tensor_tensor(h_f[b], ps[:, 6 + b, :], HS / WS, silu_f[b], ALU.mult, ALU.mult)\
                   .then_inc(hf_ready, 1)
                dve.wait_ge(hf_hi, m + 1)
                dve.tensor_tensor(h_t[b][1], h_f[b], h_t[b][0], ALU.subtract).then_inc(hf_lo, 1)

            def ffn_added(f, c):
                dve.wait_ge(df_done, CHUNKS * FB * f + FB * c + FB)
                for j in range(CH):
                    xt = x[:, bass.ds(CH * c + j, 1), :].rearrange("p a n -> p (a n)")
                    dve.scalar_tensor_tensor(xt, ps[:, j, :], 1.0 / (HS * WS), xt, ALU.mult, ALU.add)\
                       .then_inc(df_added, 1)

            def ffn_chunk(f, c):
                i = 2 * CHUNKS * f + c
                m0 = CHUNKS * FB * f + FB * c
                ln_low(i)
                with dve.Fori(0, FB // 2 - 2) as k:
                    for b in range(2):
                        ffn_product(m0 + 2 * k + b, b)
                st = ln_steps(i + 1)
                ffn_product(m0 + FB - 4, 0)
                ln_stats(st, 1 - c, range(CH))
                ffn_product(m0 + FB - 3, 1)
                ln_rstd(st, 0, CH)
                ffn_product(m0 + FB - 2, 0)
                ln_normed(1 - c, range(2))
                ffn_product(m0 + FB - 1, 1)
                ln_normed(1 - c, range(2, CH))
                ffn_added(f, c)

            last = PAIRS - 1
            ln_low(0)
            for ib in range(FB):
                ffn_product(ib, ib % 2)
                if ib < COUNTS:
                    look(last, ib)
                if ib == COUNTS:
                    finish(last)
                if ib == COUNTS + 1:
                    verify(last)
                if ib == COUNTS + 2:
                    prune(TILES - 2)
                if ib == COUNTS + 3:
                    prune(TILES - 1)
                if ib == COUNTS + 4:
                    ln_stats(sel, 1, range(2))
                    ln_rstd(sel, 0, 2)
                if ib == COUNTS + 5:
                    ln_normed(1, range(2))
            ffn_added(0, 0)
            for g in range(GB):
                fill_h(g, 4 + g)
            for g in range(GB):
                fill_h(g, 4 + g)
                if g == GB - 2:
                    down_added(TILES - 2, DO)
                    dve.wait_ge(da_added, TILES - 1)
                    ln_stats(sel, 1, range(2, 3))
            ln_rstd(sel, 2, 3)
            ln_normed(1, range(2, 3))
            down_added(TILES - 1, 0)
            dve.wait_ge(da_added, TILES)
            ln_stats(sel, 1, range(3, 4))
            ln_rstd(sel, 3, 4)
            ln_normed(1, range(3, 4))
            ffn_chunk(0, 1)
            dve.wait_ge(bias_loaded, 16)
            with dve.Fori(0, CHUNKS) as b:
                ln_low(CHUNKS + b)
                for n in range(9):
                    if n < 8:
                        i = QK_ORDER[n]
                        dve.wait_ge(qk_mm, 8 * b + n + 1)
                        if n >= 2:
                            dve.wait_ge(qk_lo, 8 * b + n - 1)
                        dve.tensor_scalar(qk_full[n % 2], ps[:, n % 4, :], 1.0 / WS, bias_qk[:, i:i + 1],
                                          ALU.mult, ALU.add).then_inc(qk_biased, 1)
                    if n >= 1:
                        i = QK_ORDER[n - 1]
                        dve.wait_ge(qk_hi, 8 * b + n)
                        dve.tensor_tensor(qk_part[:, i, 1, :], qk_full[(n - 1) % 2], qk_part[:, i, 0, :],
                                          ALU.subtract).then_inc(qk_lo, 1)
                dve.wait_ge(qk_lo, 8 * b + 8)
                def values():
                    for j in range(CH):
                        dve.wait_ge(v_mm, CH * b + j + 1)
                        dve.scalar_tensor_tensor(v_heads[:, j, :, 0:HD],
                                                 ps[:, 2 + j, :].rearrange("p (h d) -> p h d", h=HEADS), 1.0 / WS,
                                                 bias_v.rearrange("p (h d) -> p h d", h=HEADS),
                                                 ALU.mult, ALU.add).then_inc(v_ready, 1)
                    dve.memset(v_heads[:, :, :, HD], 1.0 / CS).then_inc(v_ones, 1)
                    dve.memset(v_aug[:, :, HEADS * HD1:VW], 0.0).then_inc(v_ones, 1)

                def maxes(s, qt):
                    if s < SLOTS:
                        for j in range(2):
                            dve.wait_ge(s1_full, 8 * SLOTS * b + 8 * s + 2 * qt + j + 1)
                            dve.tensor_reduce(maxima[:, qt, 2 * s + j:2 * s + j + 1], ps[:, j, :], AX, ALU.max)\
                               .then_inc(max_done, 1)

                def normalise(s):
                    st = Steps(dve, ctx_step)
                    st.base = SLOTS * b + s
                    dve.wait_ge(w_turned, SLOTS * b + s + 1)
                    turned = ps[:, 7, 0:2 * 32 * CH].rearrange("p (t j d) -> p t j d", j=2, d=32)
                    st.did(dve.reciprocal(recip[:, :].rearrange("p (t j) -> p t j", j=2), turned[:, :, :, HD]))
                    st.settle()
                    cols = 2 * HD * (s % 4)
                    dst = context[:, s // 4, :, cols:cols + 2 * HD].rearrange("p t (j d) -> p t j d", j=2)
                    dve.tensor_tensor(dst, turned[:, :, :, 0:HD],
                                      recip[:, :].rearrange("p (t j) -> p t j", j=2).unsqueeze(3)
                                      .to_broadcast([P, CH, 2, HD]), ALU.mult).then_inc(ctx_done, 1)

                for u in range(SLOTS + LAG + 1):
                    if u == LAG:
                        values()
                    for qt in range(3):
                        maxes(u, qt)
                    if u > LAG:
                        normalise(u - LAG - 1)
                    maxes(u, 3)
                    if u == SLOTS:
                        st = ln_steps(CHUNKS + b + 1)
                        ln_stats(st, 1 - b, range(CH))
                    if u == SLOTS + 2:
                        ln_rstd(st, 0, CH)
                for j in range(CH):
                    cols = slice(j * P, (j + 1) * P)
                    dve.wait_ge(ct_hi, CH * b + j + 1)
                    dve.tensor_tensor(x_t[1][:, :, cols], ps[:, 4 + j, :].rearrange("p (a q) -> p a q", q=P),
                                      x_t[0][:, :, cols], ALU.subtract).then_inc(ct_lo, 1)
                ln_normed(1 - b, range(CH))
                for j in range(CH):
                    xt = x[:, bass.ds(CH * b + j, 1), :].rearrange("p a n -> p (a n)")
                    dve.wait_ge(o_full, CH * b + j + 1)
                    dve.scalar_tensor_tensor(xt, ps[:, j, :], 1.0 / (CS * WS), xt, ALU.mult, ALU.add)\
                       .then_inc(o_step, 1)
                    dve.wait_ge(o_step, CH * b + j + 1)
                    dve.tensor_tensor(xt, xt, bias_o, ALU.add).then_inc(o_added, 1)
            with dve.Fori(0, CHUNKS) as c:
                ffn_chunk(1, c)

        @block.tensor
        def _(pe):
            def mm3(dst, st, mv, first, last):
                pe.matmul(dst, st[0], mv[0], start=first, stop=False)
                pe.matmul(dst, st[0], mv[1], start=False, stop=False)
                return pe.matmul(dst, st[1], mv[0], start=False, stop=last)

            fills = [0]

            def fill(blocks, bank=TR):
                if fills[0] >= 1 and bank == TR:
                    pe.wait_ge(tr_lo, fills[0])
                for i, blk in enumerate(blocks):
                    last = pe.transpose(ps[:, bank, i * P:(i + 1) * P], blk, ident[:, :])
                last.then_inc(tr_full, 1)
                fills[0] += 1

            def normed(t):
                pe.wait_ge(xa_norm, t + 1)
                fill([xn_a[:, hb * P:(hb + 1) * P] for hb in range(HB)])

            def project(w, bank, t):
                j = t % 2
                for hb in range(HB):
                    if t == 0:
                        pe.wait_ge(wa_lo, hb + 1 + (HB if bank else 0))
                    for c in range(3):
                        a, e = c * 512, min(IA, (c + 1) * 512)
                        last = mm3(psf[:, bank * 512 + a:bank * 512 + e],
                                   [q[:, hb, j * P:(j + 1) * P] for q in xa_t], [q[:, hb, a:e] for q in w],
                                   hb == 0, hb == HB - 1)
                return last

            def turn(n, j, g, bank):
                k, w = 4 * g, min(4, AB - 4 * g)
                fill([prod[n % 2][:, j, (k + i) * P:(k + i + 1) * P] for i in range(w)], bank)

            def pair_down(n, banks, out0, out1):
                f0 = fills[0]

                def part(g, bank):
                    for k in range(4 * g, min(AB, 4 * g + 4)):
                        mm = mm3(ps[:, bank, :], [q[:, k, :] for q in ha_t], [q[:, k, :] for q in da],
                                 k == 0, k == AB - 1)
                    if g == GB - 1:
                        mm.then_inc(da_full, 1)

                pe.wait_ge(pruned, 2 * n + 1)
                for g in range(GB):
                    turn(n, 0, g, banks[g])
                for g in range(GB):
                    pe.wait_ge(tr_lo, f0 + g + 1)
                    part(g, out0)
                    if g == 0:
                        pe.wait_ge(pruned, 2 * n + 2)
                    turn(n, 1, g, banks[g])
                for g in range(GB):
                    pe.wait_ge(tr_lo, f0 + GB + g + 1)
                    part(g, out1)

            pe.wait_ge(const_ready, 1)
            for t in range(2):
                normed(t)
            for n in range(PAIRS):
                pe.wait_ge(tr_lo, fills[0])
                for j in range(2):
                    t = 2 * n + j
                    if t >= 1:
                        pe.wait_ge(ga_silu, t)
                    project(ga, 0, t).then_inc(ga_full, 1)
                    if t >= 1:
                        pe.wait_ge(ua_used, t)
                    project(ua, 3, t).then_inc(ua_full, 1)
                    if n + 1 < PAIRS:
                        if n >= 2:
                            pe.wait_ge(da_added, 2 * n - 2)
                        normed(t + 2)
                if n >= 1:
                    if n == 1:
                        pe.wait_ge(pads_zero, 4)
                        pe.wait_ge(wa_lo, 2 * HB + 2)
                    else:
                        pe.wait_ge(da_added, 2 * n - 2)
                    pe.wait_ge(ga_silu, 2 * n + 2)
                    pe.wait_ge(tr_lo, fills[0])
                    pair_down(n - 1, (0, 1, 2), DO, TR)

            def norm(i):
                for j in range(CH):
                    pe.wait_ge(ln_norm, CH * i + j + 1)
                    for hb in range(HB):
                        last = pe.transpose(ps[:, 4 + j, hb * P:(hb + 1) * P], xn[j][:, hb * P:(hb + 1) * P],
                                            ident[:, :])
                    last.then_inc(ln_full, 1)
                pe.wait_ge(ln_lo, CH * i + CH)

            def ffn_chunk(f, c):
                m0 = CHUNKS * FB * f + FB * c

                def gate_up(ib, b, reuse):
                    cols = bass.ds(ib * P, P)
                    for w, bank, full, used in ((fg, 4 + b, gf_full, gf_silu), (fu, 6 + b, uf_full, hf_ready)):
                        if reuse:
                            pe.wait_ge(used, m0 + ib - 1)
                        for hb in range(HB):
                            last = mm3(ps[:, bank, :], [q[:, hb, cols] for q in w], [q[:, hb, :] for q in x_t],
                                       hb == 0, hb == HB - 1)
                        last.then_inc(full, 1)

                def down(ib, b, first, last):
                    pe.wait_ge(hf_lo, m0 + ib + 1)
                    if f == 0:
                        pe.wait_ge(q_lo, N_GU + (H // CW) * (ib + 1))
                    row = [q[:, bass.ds(ib, 1), :].rearrange("p a n -> p (a n)") for q in fd]
                    for j in range(CH):
                        mm = mm3(ps[:, j, :], [q[:, j * P:(j + 1) * P] for q in h_t[b]], row, first, last)
                    mm.then_inc(df_done, 1)

                norm(2 * CHUNKS * f + c)
                if f == 0:
                    pe.wait_ge(q_lo, N_GU)
                gate_up(0, 0, False)
                gate_up(1, 1, False)
                down(0, 0, True, False)
                with pe.Fori(1, FB // 2) as k:
                    gate_up(2 * k, 0, True)
                    down(2 * k - 1, 1, False, False)
                    gate_up(2 * k + 1, 1, True)
                    down(2 * k, 0, False, False)
                down(FB - 1, 1, False, True)

            pe.wait_ge(ga_silu, TILES)
            pe.wait_ge(ua_used, TILES)
            pe.wait_ge(da_added, TILES - 2)
            ffn_chunk(0, 0)
            pe.wait_ge(df_added, CH)
            pair_down(PAIRS - 1, (4, 5, 6), DO, 0)
            pe.wait_ge(da_added, TILES)
            ffn_chunk(0, 1)

            pe.wait_ge(aw_lo, 2)
            pe.wait_ge(fold_ready, 1)
            with pe.Fori(0, CHUNKS) as b:
                norm(CHUNKS + b)
                for n, i in enumerate(QK_ORDER):
                    if n >= 4:
                        pe.wait_ge(qk_biased, 8 * b + n - 3)
                    for hb in range(HB):
                        last = mm3(ps[:, n % 4, :], [q[:, hb, i * P:(i + 1) * P] for q in wqkv],
                                   [q[:, hb, :] for q in x_t], hb == 0, hb == HB - 1)
                    last.then_inc(qk_mm, 1)
                pe.wait_ge(qk_biased, 8 * b + 8)
                pe.wait_ge(stacked[0], 512 * b + 512)
                pe.wait_ge(stacked_pool[0], 256 * b + 256)

                def values():
                    for j in range(CH):
                        for hb in range(HB):
                            last = mm3(ps[:, 2 + j, :], [q[:, hb, j * P:(j + 1) * P] for q in x_t],
                                       [q[:, hb, 2 * H:3 * H] for q in wqkv], hb == 0, hb == HB - 1)
                        last.then_inc(v_mm, 1)

                def scores(s, qt):
                    if s < SLOTS:
                        if s == SLOTS // 2 and qt == 0:
                            pe.wait_ge(stacked[1], 512 * b + 512)
                            pe.wait_ge(stacked_pool[1], 256 * b + 256)
                        for j in range(2):
                            r = 8 * s + 2 * qt + j
                            if r >= 2:
                                pe.wait_ge(max_done, 8 * SLOTS * b + r - 1)
                            rows = slice(64 * j, 64 * j + 3 * HD)
                            pe.matmul(ps[:, j, :], q_st[rows, s, qt * P:(qt + 1) * P], k_st[rows, s, :],
                                      start=True, stop=True).then_inc(s1_full, 1)

                def turn_maxima(g, slots):
                    if slots:
                        pe.wait_ge(ctx_done, SLOTS * b + slots)
                    pe.wait_ge(max_done, 8 * SLOTS * b + 8 * GS * (g + 1))
                    if g >= 1:
                        pe.wait_ge(mt_ready, GROUPS * b + g)
                    for qt in range(CH):
                        last = pe.transpose(ps[0:2 * GS, 7, qt * P:(qt + 1) * P],
                                            maxima[:, qt, 2 * GS * g:2 * GS * (g + 1)], ident[:, :])
                    last.then_inc(mt_full, 1)

                def scores_t(s, half):
                    if s % GS == 0 and half == 0:
                        pe.wait_ge(max_moved[s // GS], 32 * b + 32)
                    for j in range(2):
                        e = 4 * s + 2 * half + j
                        if e >= 2:
                            pe.wait_ge(exp_done, 4 * SLOTS * b + e - 1)
                    for kk in range(2):
                        for j in range(2):
                            rows = slice(64 * j, 64 * j + 3 * HD + 1)
                            kb = 2 * half + kk
                            mm = pe.matmul(ps[:, 2 + 2 * j + kk, :], k_st[rows, s, kb * P:(kb + 1) * P],
                                           q_st[rows, s, :], start=True, stop=True)
                            if kk == 1:
                                mm.then_inc(s2_full, 1)

                def weigh(s, half):
                    pe.wait_ge(exp_done, 4 * SLOTS * b + 4 * s + 2 * half + 2)
                    if half == 0 and s >= 1:
                        pe.wait_ge(wt_ready, SLOTS * b + s)
                    for j in range(2):
                        for kk in range(2):
                            part = slice(32 * (2 * j + kk), 32 * (2 * j + kk + 1))
                            at, kb = (2 * s + j) * HD1, 2 * half + kk
                            mm = pe.matmul(ps[part, 6, :], v_aug[:, kb, at:at + 32], probs[:, j, kb, :],
                                           start=(half == 0), stop=(half == 1))
                    mm.then_inc(pv_done, 1)

                def turn_weighted(s, turned):
                    pe.wait_ge(wt_ready, SLOTS * b + s + 1)
                    if s >= 1:
                        pe.wait_ge(ctx_done, SLOTS * b + s)
                    if turned:
                        pe.wait_ge(mt_ready, GROUPS * b + turned)
                    for qt in range(CH):
                        mm = pe.matmul(ps[:, 7, qt * 64:(qt + 1) * 64], weighted_t[:, qt * P:(qt + 1) * P],
                                       fold, start=True, stop=True)
                    mm.then_inc(w_turned, 1)

                turned = 0
                for u in range(SLOTS + LAG + 1):
                    s = u - LAG
                    if s == 0:
                        values()
                    scores(u, 0)
                    if s == 0:
                        pe.wait_ge(v_ready, CH * b + CH)
                        pe.wait_ge(v_ones, 2 * b + 2)
                    if 0 <= s < SLOTS:
                        scores_t(s, 0)
                    if u >= GS and u % GS == 0 and u // GS <= GROUPS:
                        turn_maxima(turned, max(0, s - 1))
                        turned += 1
                    scores(u, 1)
                    if s >= 1:
                        weigh(s - 1, 1)
                    scores(u, 2)
                    if 0 <= s < SLOTS:
                        scores_t(s, 1)
                    if s >= 1:
                        turn_weighted(s - 1, turned)
                    scores(u, 3)
                    if 0 <= s < SLOTS:
                        weigh(s, 0)

                pe.wait_ge(ctx_done, SLOTS * b + SLOTS)
                for j in range(CH):
                    for i in range(HB):
                        last = pe.transpose(ps[:, 4 + j, i * P:(i + 1) * P], context[:, i, j, :], ident[:, :])
                    last.then_inc(ct_full, 1)
                for j in range(CH):
                    pe.wait_ge(ct_lo, CH * b + j + 1)
                    for hb in range(HB):
                        last = mm3(ps[:, j, :], [q[:, hb, j * P:(j + 1) * P] for q in x_t],
                                   [q[:, hb, :] for q in wo], hb == 0, hb == HB - 1)
                    last.then_inc(o_full, 1)
            with pe.Fori(0, CHUNKS) as c:
                ffn_chunk(1, c)


def kernel(**inputs):
    import numpy as np
    import concourse.bacc as bacc
    from concourse.bass_utils import run_bass_kernel_spmd

    a = {k.removeprefix("L0_"): np.asarray(v) for k, v in inputs.items()}
    shape = a["attn_a_x"].shape
    laid = {
        "x": a["attn_a_x"].reshape(-1, shape[-1]),
        "w_gate_t": a["attn_a_w_gate"].T, "w_up_t": a["attn_a_w_up"].T, "w_down_t": a["attn_a_w_down"].T,
        "qkvw": a["attn_b_attn_qkvw"], "qkvb": a["attn_b_attn_qkvb"],
        "ow": a["attn_b_attn_ow"], "ob": a["attn_b_attn_ob"],
    }
    for m in ("gate", "up", "down"):
        for part in "wzs":
            laid[f"{m}_{part}"] = a[f"ffn_{m}_{part}"]
    nc = bacc.Bacc("TRN2", target_bir_lowering=False, num_devices=1)
    arrays, args = {}, []
    for name, v in laid.items():
        v = np.ascontiguousarray(v)
        arrays[f"in_{name}"] = v
        args.append(nc.dram_tensor(f"in_{name}", v.shape, mybir.dt.from_np(v.dtype), kind="ExternalInput").ap())
    args.append(nc.dram_tensor("out_x", laid["x"].shape, F32, kind="ExternalOutput").ap())
    hybrid_layers(nc, *args)
    r = run_bass_kernel_spmd(nc, [arrays], core_ids=[0])
    return r.results[0]["out_x"].reshape(shape)
```
